# Optimizing a Trainium2 kernel written in Bass

```python
import numpy as np
import jax
import jax.numpy as jnp

def _softmax(x, axis=-1):
    return jax.nn.softmax(x, axis=axis)

def _gelu(x):
    return jax.nn.gelu(x, approximate=True)

def _silu(x):
    return jax.nn.silu(x)

def _sigmoid(x):
    return jax.nn.sigmoid(x)

def _layernorm(x, axis=-1, eps=1e-05):
    m = jnp.mean(x, axis=axis, keepdims=True)
    v = jnp.var(x, axis=axis, keepdims=True)
    return (x - m) / jnp.sqrt(v + eps)

def _scatter_add(tgt, idx, src, axis=0):
    return tgt.at[idx].add(src)

def _segment_sum(src, seg, n):
    return jax.ops.segment_sum(src, seg, n)
kernel_name = 'mk_xattn_seq_d1_seqx_r4_8f010a'

def setup_inputs(seed: int=0):
    np.random.seed(seed)
    _w = jnp.asarray

    def _rec_inputs():
        import jax
        import jax.numpy as jnp
        _rk = jax.random.key(seed)
        x = -0.0003929 + 0.9999 * jax.random.normal(jax.random.fold_in(_rk, 1), (4, 512, 1024), jnp.float32)
        _lenS = 512 - jax.random.randint(jax.random.fold_in(_rk, 7), (4,), 0, max(1, 512 // 4) + 1, jnp.int32)
        _lenS2 = 1601 - jax.random.randint(jax.random.fold_in(_rk, 8), (4,), 0, max(1, 1601 // 4) + 1, jnp.int32)
        _ctx_4096P = jax.random.normal(jax.random.fold_in(_rk, 11), (4, 16, 1024), jnp.float32)
        _ctx_4096c = jax.random.dirichlet(jax.random.fold_in(_rk, 511), 0.3 * jnp.ones((16,), jnp.float32), (4, 1601))
        _ctx_4096t = jnp.einsum('bsk,bkd->bsd', _ctx_4096c, _ctx_4096P)
        _ctx_4096t = _ctx_4096t * jax.lax.rsqrt(jnp.mean(jnp.square(_ctx_4096t)) + 1e-12) * 0.953939
        ctx_4096 = 2.81802e-05 + 1.00001 * (_ctx_4096t + 0.3 * jax.random.normal(jax.random.fold_in(_rk, 611), (4, 1601, 1024), jnp.float32))
        return (x, ctx_4096)
    x, ctx_4096 = _rec_inputs()

    def _L0_xattn_setup():
        import jax, jax.numpy as jnp
        import numpy as np
        H = 1024
        NH = 32
        NKV = 8
        HD = H // NH
        R = 16
        SCALING = 32.0 / 16.0

        def _lora_linear(x, W, A, B):
            return x @ W + SCALING * (x @ A @ B)
        key = jax.random.key(seed)
        ks = jax.random.split(key, 16)
        d = {'hidden_states': jax.random.normal(ks[0], (4, 256, H), jnp.float32), 'traces': jax.random.normal(ks[1], (4, 256, H), jnp.float32), 'Wq': jax.random.normal(ks[2], (H, H), jnp.float32) * 0.02, 'Aq': jax.random.normal(ks[3], (H, R), jnp.float32) * 0.02, 'Bq': jax.random.normal(ks[4], (R, H), jnp.float32) * 0.02, 'Wk': jax.random.normal(ks[5], (H, NKV * HD), jnp.float32) * 0.02, 'Ak': jax.random.normal(ks[6], (H, R), jnp.float32) * 0.02, 'Bk': jax.random.normal(ks[7], (R, NKV * HD), jnp.float32) * 0.02, 'Wv': jax.random.normal(ks[8], (H, NKV * HD), jnp.float32) * 0.02, 'Av': jax.random.normal(ks[9], (H, R), jnp.float32) * 0.02, 'Bv': jax.random.normal(ks[10], (R, NKV * HD), jnp.float32) * 0.02, 'Wo': jax.random.normal(ks[11], (H, H), jnp.float32) * 0.02, 'Ao': jax.random.normal(ks[12], (H, R), jnp.float32) * 0.02, 'Bo': jax.random.normal(ks[13], (R, H), jnp.float32) * 0.02}
        return d
    _L0_xattn_all = _L0_xattn_setup()
    _L0_xattn_in = {k: v for k, v in _L0_xattn_all.items() if k in ('Wq', 'Aq', 'Bq', 'Wk', 'Ak', 'Bk', 'Wv', 'Av', 'Bv', 'Wo', 'Ao', 'Bo')}
    del _L0_xattn_all
    return {'x': x, 'ctx_4096': ctx_4096, 'L0_xattn_Wq': _L0_xattn_in['Wq'], 'L0_xattn_Aq': _L0_xattn_in['Aq'], 'L0_xattn_Bq': _L0_xattn_in['Bq'], 'L0_xattn_Wk': _L0_xattn_in['Wk'], 'L0_xattn_Ak': _L0_xattn_in['Ak'], 'L0_xattn_Bk': _L0_xattn_in['Bk'], 'L0_xattn_Wv': _L0_xattn_in['Wv'], 'L0_xattn_Av': _L0_xattn_in['Av'], 'L0_xattn_Bv': _L0_xattn_in['Bv'], 'L0_xattn_Wo': _L0_xattn_in['Wo'], 'L0_xattn_Ao': _L0_xattn_in['Ao'], 'L0_xattn_Bo': _L0_xattn_in['Bo']}

def reference(x, ctx_4096, L0_xattn_Wq, L0_xattn_Aq, L0_xattn_Bq, L0_xattn_Wk, L0_xattn_Ak, L0_xattn_Bk, L0_xattn_Wv, L0_xattn_Av, L0_xattn_Bv, L0_xattn_Wo, L0_xattn_Ao, L0_xattn_Bo):
    import jax
    import jax.numpy as jnp

    def _L0_xattn_ref(hidden_states, traces, Wq, Aq, Bq, Wk, Ak, Bk, Wv, Av, Bv, Wo, Ao, Bo):
        import jax, jax.numpy as jnp
        import numpy as np
        H = 1024
        NH = 32
        NKV = 8
        HD = H // NH
        R = 16
        SCALING = 32.0 / 16.0

        def _lora_linear(x, W, A, B):
            return x @ W + SCALING * (x @ A @ B)
        bsz, q_len, _ = hidden_states.shape
        t_len = traces.shape[1]
        groups = NH // NKV
        q = _lora_linear(hidden_states, Wq, Aq, Bq).reshape(bsz, q_len, NH, HD)
        q = jnp.transpose(q, (0, 2, 1, 3))
        k = _lora_linear(traces, Wk, Ak, Bk).reshape(bsz, t_len, NKV, HD)
        v = _lora_linear(traces, Wv, Av, Bv).reshape(bsz, t_len, NKV, HD)
        k = jnp.transpose(k, (0, 2, 1, 3))
        v = jnp.transpose(v, (0, 2, 1, 3))
        k = jnp.repeat(k, groups, axis=1)
        v = jnp.repeat(v, groups, axis=1)
        scores = jnp.einsum('bhqd,bhtd->bhqt', q, k) / jnp.sqrt(jnp.asarray(HD, q.dtype))
        attn = jax.nn.softmax(scores, axis=-1)
        context = jnp.einsum('bhqt,bhtd->bhqd', attn, v)
        context = jnp.transpose(context, (0, 2, 1, 3)).reshape(bsz, q_len, H)
        out = _lora_linear(context, Wo, Ao, Bo)
        return hidden_states + out
    x = _L0_xattn_ref(x, ctx_4096, L0_xattn_Wq, L0_xattn_Aq, L0_xattn_Bq, L0_xattn_Wk, L0_xattn_Ak, L0_xattn_Bk, L0_xattn_Wv, L0_xattn_Av, L0_xattn_Bv, L0_xattn_Wo, L0_xattn_Ao, L0_xattn_Bo)
    return x

_drawn_inputs = setup_inputs


def setup_inputs(seed=0):
    import zlib

    import numpy as np

    out = dict(_drawn_inputs(seed))
    spreads = {}
    factors = {'L0_xattn_Aq': 8.0, 'L0_xattn_Bq': 8.0, 'L0_xattn_Ak': 8.0, 'L0_xattn_Bk': 8.0}
    for name, (base, spread) in spreads.items():
        noise = np.random.default_rng([zlib.crc32(name.encode()), seed]).standard_normal(out[name].shape)
        drawn = base * np.exp(spread * noise) if base else spread * noise
        out[name] = jnp.asarray(drawn.astype(out[name].dtype))
    for name, factor in factors.items():
        out[name] = (out[name] * factor).astype(out[name].dtype)
    return out
```

```python
from contextlib import ExitStack

import numpy as np
import concourse.bass as bass
from concourse import mybir

F32 = mybir.dt.float32
F32R = mybir.dt.float32r
ALU = mybir.AluOpType
ACT = mybir.ActivationFunctionType
AX = mybir.AxisListType

B, Q, T, H = 4, 512, 1601, 1024
NH, NKV, R = 32, 8, 16
HD = H // NH
KV = NKV * HD
GH = NH // NKV
NG = B * NKV
LORA_SCALE = 2.0
P = 128
KT = H // P
NT = -(-T // P)
TP = NT * P
TL = T - (NT - 1) * P
BANK = 512
SCALE = float(HD) ** -0.5
TERMS = ((0, 0), (1, 0), (0, 1))


def fold_weights(nc, ctx, name, cols, pairs, done_sem):
    at = ctx.enter_context(nc.sbuf_tensor(f"{name}_at", [R, len(pairs), H], F32))
    lb = ctx.enter_context(nc.sbuf_tensor(f"{name}_lb", [R, cols], F32))
    raw = ctx.enter_context(nc.sbuf_tensor(f"{name}_raw", [P, KT, cols], F32))
    parts = ctx.enter_context(nc.sbuf_tensor(f"{name}_parts", [P, 2, KT, cols], F32R))
    loaded = ctx.enter_context(nc.semaphore(f"{name}_loaded"))
    ab_ready = ctx.enter_context(nc.semaphore(f"{name}_ab_ready"))
    summed = ctx.enter_context(nc.semaphore(f"{name}_summed"))
    hi_done = ctx.enter_context(nc.semaphore(f"{name}_hi_done"))
    units = [(k, c) for k in range(KT) for c in range(0, cols, BANK)]

    def load(sp):
        for j, (a, b, w, c0) in enumerate(pairs):
            n = b.shape[1]
            sp.dma_start(at[:, j, :], a).then_inc(loaded, 16)
            sp.dma_start(lb[:, c0:c0 + n], b).then_inc(loaded, 16)
            sp.dma_start(raw[:, :, c0:c0 + n], w.rearrange("(k p) n -> p k n", p=P)).then_inc(loaded, 16)

    def all_loaded(eng):
        eng.wait_ge(loaded, 48 * len(pairs))

    def products(pe, banks):
        all_loaded(pe)
        for u, (k, c) in enumerate(units):
            if u >= len(banks):
                pe.wait_ge(summed, u - len(banks) + 1)
            for j, (_, b, _, c0) in enumerate(pairs):
                lo, hi = max(c, c0), min(c + BANK, c0 + b.shape[1])
                if lo < hi:
                    last = nc.tensor.matmul(banks[u % len(banks)][:, lo - c:hi - c], at[:, j, k * P:(k + 1) * P],
                                            lb[:, lo:hi], start=True, stop=True)
            last.then_inc(ab_ready, 1)

    def high_parts(act):
        for u, (k, c) in enumerate(units):
            act.wait_ge(summed, u + 1)
            nc.scalar.activation(parts[:, 0, k, c:c + BANK], raw[:, k, c:c + BANK], ACT.Copy).then_inc(hi_done, 1)

    def sums_and_low_parts(dve, banks):
        all_loaded(dve)

        def low(u):
            k, c = units[u]
            dve.wait_ge(hi_done, u + 1)
            nc.vector.tensor_tensor(parts[:, 1, k, c:c + BANK], raw[:, k, c:c + BANK],
                                    parts[:, 0, k, c:c + BANK].bitcast(F32), ALU.subtract).then_inc(done_sem, 1)

        for u, (k, c) in enumerate(units):
            dve.wait_ge(ab_ready, u + 1)
            nc.vector.scalar_tensor_tensor(out=raw[:, k, c:c + BANK], in0=banks[u % len(banks)][:, :],
                                           scalar=LORA_SCALE, in1=raw[:, k, c:c + BANK],
                                           op0=ALU.mult, op1=ALU.add).then_inc(summed, 1)
            if u >= 1:
                low(u - 1)
        low(len(units) - 1)

    return parts, len(units), load, products, high_parts, sums_and_low_parts


def keys_and_values(nc, ctxT, wk, ak, bk, wv, av, bv, k_scr, v_scr):
    widths = [min(BANK, TP - t) for t in range(0, TP, BANK)]
    NC = len(widths)
    assert NC % 2 == 0
    ends = [min((c + 1) * BANK, TP) // P for c in range(NC)]
    MK = KV // P
    with ExitStack() as ctx:
        sb = lambda n, s, d: ctx.enter_context(nc.sbuf_tensor(n, s, d))
        sem = lambda n: ctx.enter_context(nc.semaphore(n))
        w_done = sem("wkv_done")
        w, w_units, w_load, w_products, w_high, w_low = fold_weights(
            nc, ctx, "wkv", 2 * KV, [(ak, bk, wk, 0), (av, bv, wv, KV)], w_done)
        raw = [sb(f"ctx_raw{i}", [P, KT, BANK], F32) for i in range(2)]
        parts = [sb(f"ctx_parts{i}", [P, 2, KT, BANK], F32R) for i in range(2)]
        k_out = [sb(f"k_out{i}", [P, 2, BANK], F32R) for i in range(MK)]
        v_out = sb("v_out", [P, NKV, NT, HD], F32)
        banks = [ctx.enter_context(nc.psum_tensor(f"kv_bank{i}", [P, BANK], F32)) for i in range(8)]
        k_bank, v_bank = banks[0:4], banks[4:8]
        ctx_loaded = [sem(f"ctx_loaded{i}") for i in range(2)]
        ctx_hi, ctx_lo = sem("ctx_hi"), sem("ctx_lo")
        k_ready, k_hi, k_lo = sem("k_ready"), sem("k_hi"), sem("k_lo")
        v_ready, v_copied = sem("v_ready"), sem("v_copied")
        k_stored, v_stored = [sem(f"k_stored{i}") for i in range(MK)], sem("v_stored")
        block = ctx.enter_context(nc.Block())

        def v_tiles_before(b, c):
            return b * NT + (ends[c - 2] + NT if c >= 2 else ends[c - 2])

        @block.sync
        def _(sp):
            def load(b, c):
                sp.wait_ge(ctx_lo, b * NC + c - 1 + NC)
                sp.dma_start(raw[c % 2][:, :, 0:widths[c]],
                             ctxT[bass.ds(b, 1), :, c * BANK:c * BANK + widths[c]].rearrange(
                                 "o (k p) t -> (o p) k t", p=P)).then_inc(ctx_loaded[c % 2], 16)

            def batch(b, last):
                for c in range(NC):
                    if c + 1 < NC:
                        load(b, c + 1)
                    elif not last:
                        load(b + 1, 0)
                    for m in range(MK):
                        sp.wait_ge(k_lo, b * (NC * MK) + c * MK + m + 1 + 4)
                        sp.dma_start(k_scr[bass.ds(b * KV + m * P, P), :, c * BANK:c * BANK + widths[c]],
                                     k_out[m][:, :, 0:widths[c]].bitcast(F32)).then_inc(k_stored[m], 16)
                sp.wait_ge(v_copied, (b + 2) * NT)
                sp.dma_start(v_scr[bass.ds(b * NKV, NKV), :, :].rearrange("g p f -> p g f"),
                             v_out[:, :, :, :].rearrange("p g t d -> p g (t d)")).then_inc(v_stored, 16)

            w_load(sp)
            load(0, 0)
            with sp.Fori(0, B - 1) as b:
                batch(b, False)
            batch(B - 1, True)
            for m in range(MK):
                sp.wait_ge(k_stored[m], (B * NC + 1) * 16)
            sp.wait_ge(v_stored, (B + 1) * 16)

        @block.scalar
        def _(act):
            act.sem_inc(v_copied, NT)
            for m in range(MK):
                act.sem_inc(k_stored[m], 16)
            act.sem_inc(v_stored, 16)
            w_high(act)
            with act.Fori(0, B) as b:
                for c in range(NC):
                    n = widths[c]
                    act.wait_ge(ctx_loaded[c % 2], (b * (NC // 2) + c // 2 + 1) * 16)
                    act.wait_ge(v_ready, v_tiles_before(b, c))
                    nc.scalar.activation(parts[c % 2][:, 0, :, 0:n], raw[c % 2][:, :, 0:n], ACT.Copy).then_inc(ctx_hi, 1)
                    for m in range(MK):
                        u = b * (NC * MK) + c * MK + m
                        act.wait_ge(k_ready, u + 1)
                        act.wait_ge(k_stored[m], (b * NC + c + 1) * 16)
                        nc.scalar.activation(k_out[m][:, 0, 0:n], k_bank[(c * MK + m) % 4][:, 0:n],
                                             ACT.Copy).then_inc(k_hi, 1)
                    for t in range(ends[c - 1] if c else 0, ends[c]):
                        act.wait_ge(v_ready, b * NT + t + 1 + NT)
                        if t == 0:
                            act.wait_ge(v_stored, (b + 1) * 16)
                        nc.scalar.activation(v_out[:, :, t, :],
                                             v_bank[t % 4][:, 0:KV].rearrange("p (g d) -> p g d", g=NKV),
                                             ACT.Copy).then_inc(v_copied, 1)

        @block.vector
        def _(dve):
            dve.sem_inc(ctx_lo, NC)
            dve.sem_inc(k_lo, 4)
            w_low(dve, banks)
            with dve.Fori(0, B) as b:
                for c in range(NC):
                    n = widths[c]
                    dve.wait_ge(ctx_hi, b * NC + c + 1)
                    nc.vector.tensor_tensor(parts[c % 2][:, 1, :, 0:n], raw[c % 2][:, :, 0:n],
                                            parts[c % 2][:, 0, :, 0:n].bitcast(F32),
                                            ALU.subtract).then_inc(ctx_lo, 1)
                    for m in range(MK):
                        u = b * (NC * MK) + c * MK + m
                        dve.wait_ge(k_hi, u + 1)
                        nc.vector.tensor_tensor(k_out[m][:, 1, 0:n], k_bank[(c * MK + m) % 4][:, 0:n],
                                                k_out[m][:, 0, 0:n].bitcast(F32), ALU.subtract).then_inc(k_lo, 1)

        @block.tensor
        def _(pe):
            pe.sem_inc(v_ready, NT)
            w_products(pe, banks)
            pe.wait_ge(w_done, w_units)
            with pe.Fori(0, B) as b:
                for c in range(NC):
                    n = widths[c]
                    x = parts[c % 2]
                    pe.wait_ge(ctx_lo, b * NC + c + 1 + NC)
                    for m in range(MK):
                        u = b * (NC * MK) + c * MK + m
                        pe.wait_ge(k_lo, u + 1)
                        for i, (k, (wp, xp)) in enumerate((k, t) for k in range(KT) for t in TERMS):
                            last = nc.tensor.matmul(k_bank[(c * MK + m) % 4][:, 0:n], w[:, wp, k, m * P:(m + 1) * P],
                                                    x[:, xp, k, 0:n], start=i == 0, stop=i == KT * len(TERMS) - 1)
                        last.then_inc(k_ready, 1)
                    for t in range(ends[c - 1] if c else 0, ends[c]):
                        t0 = t * P - c * BANK
                        used = t - 4 + NT if t >= 4 else (NT - 1 - (NT - 1 - t) % 4)
                        pe.wait_ge(v_copied, b * NT + used + 1)
                        for i, (k, (wp, xp)) in enumerate((k, t) for k in range(KT) for t in TERMS):
                            last = nc.tensor.matmul(v_bank[t % 4][:, 0:KV], x[:, xp, k, t0:t0 + P],
                                                    w[:, wp, k, KV:2 * KV], start=i == 0, stop=i == KT * len(TERMS) - 1)
                        last.then_inc(v_ready, 1)


def queries(nc, xT, wq, aq, bq, q_scr):
    MQ = H // P
    with ExitStack() as ctx:
        sb = lambda n, s, d: ctx.enter_context(nc.sbuf_tensor(n, s, d))
        sem = lambda n: ctx.enter_context(nc.semaphore(n))
        w_done = sem("wq_done")
        w, w_units, w_load, w_products, w_high, w_low = fold_weights(nc, ctx, "wq", H, [(aq, bq, wq, 0)], w_done)
        raw = sb("x_raw", [P, KT, Q], F32)
        parts = [sb(f"x_parts{i}", [P, 2, KT, Q], F32R) for i in range(2)]
        q_out = [sb(f"q_out{i}", [P, 2, Q], F32R) for i in range(2)]
        banks = [ctx.enter_context(nc.psum_tensor(f"q_bank{i}", [P, Q], F32)) for i in range(MQ)]
        x_loaded, x_hi, x_lo = sem("x_loaded"), sem("x_hi"), sem("x_lo")
        q_ready, q_hi, q_lo = sem("q_ready"), sem("q_hi"), sem("q_lo")
        q_stored = [sem(f"q_stored{i}") for i in range(2)]
        block = ctx.enter_context(nc.Block())

        def evacuations(bb, half):
            return [((bb * 2 + half) * MQ + m, m, m % 2, (bb * 2 + half) * (MQ // 2) + m // 2) for m in range(MQ)]

        @block.sync
        def _(sp):
            def load(b):
                if not (isinstance(b, int) and b == 0):
                    sp.wait_ge(x_lo, b)
                sp.dma_start(raw[:, :, :], xT[bass.ds(b, 1), :, :].rearrange(
                    "o (k p) t -> (o p) k t", p=P)).then_inc(x_loaded, 16)

            def batch(b, last):
                if not last:
                    load(b + 1)
                for m in range(MQ):
                    sp.wait_ge(q_lo, b * MQ + m + 1 + MQ)
                    sp.dma_start(q_scr[bass.ds(b * H + m * P, P), :, :],
                                 q_out[m % 2][:, :, :].bitcast(F32)).then_inc(q_stored[m % 2], 16)

            w_load(sp)
            load(0)
            with sp.Fori(0, B - 1) as b:
                batch(b, False)
            batch(B - 1, True)
            for s in range(2):
                sp.wait_ge(q_stored[s], (B * (MQ // 2) + 1) * 16)

        @block.scalar
        def _(act):
            for s in range(2):
                act.sem_inc(q_stored[s], 16)
            w_high(act)

            def split(bb, half):
                act.wait_ge(x_loaded, (bb * 2 + half + 1) * 16)
                act.wait_ge(q_ready, (bb * 2 + half + 1) * MQ)
                nc.scalar.activation(parts[half][:, 0], raw[:, :, :], ACT.Copy).then_inc(x_hi, 1)

            with act.Fori(0, B // 2) as bb:
                for half in range(2):
                    split(bb, half)
                    for u, m, s, stores in evacuations(bb, half):
                        act.wait_ge(q_ready, u + 1 + 2 * MQ)
                        act.wait_ge(q_stored[s], (stores + 1) * 16)
                        nc.scalar.activation(q_out[s][:, 0, :], banks[m][:, :], ACT.Copy).then_inc(q_hi, 1)

        @block.vector
        def _(dve):
            dve.sem_inc(q_lo, MQ)
            w_low(dve, banks)
            with dve.Fori(0, B // 2) as bb:
                for half in range(2):
                    dve.wait_ge(x_hi, bb * 2 + half + 1)
                    nc.vector.tensor_tensor(parts[half][:, 1], raw[:, :, :], parts[half][:, 0].bitcast(F32),
                                            ALU.subtract).then_inc(x_lo, 1)
                    for u, m, s, _ in evacuations(bb, half):
                        dve.wait_ge(q_hi, u + 1)
                        nc.vector.tensor_tensor(q_out[s][:, 1, :], banks[m][:, :], q_out[s][:, 0, :].bitcast(F32),
                                                ALU.subtract).then_inc(q_lo, 1)

        @block.tensor
        def _(pe):
            pe.sem_inc(q_ready, 2 * MQ)
            w_products(pe, banks)
            pe.wait_ge(w_done, w_units)
            with pe.Fori(0, B // 2) as bb:
                for half in range(2):
                    pe.wait_ge(x_lo, bb * 2 + half + 1)
                    for u, m, _, _ in evacuations(bb, half):
                        pe.wait_ge(q_lo, u + 1)
                        for i, (k, (wp, xp)) in enumerate((k, t) for k in range(KT) for t in TERMS):
                            last = nc.tensor.matmul(banks[m][:, :], w[:, wp, k, m * P:(m + 1) * P],
                                                    parts[half][:, xp, k, :], start=i == 0,
                                                    stop=i == KT * len(TERMS) - 1)
                        last.then_inc(q_ready, 1)


def attention(nc, k_scr, v_scr, q_scr, a_scr):
    S3 = 3 * HD
    QT = Q // P
    UNITS = GH * QT
    CH = 402
    NCH = 4
    assert CH % 2 == 0 and T <= NCH * CH <= TP
    PAIRS = UNITS * NCH // 2
    NS = 3
    LAST_SLOT = 11
    SHARE = [PAIRS * s // LAST_SLOT for s in range(LAST_SLOT + 1)] + [PAIRS] * (NT - LAST_SLOT)
    KP = NT // 2
    TILES = GH * NT
    SB = KP + 1
    BODY = 3
    PE_LOOPS = (NG - 2) // BODY
    SP_LOOPS = (NG - NS) // BODY

    with ExitStack() as ctx:
        sb = lambda n, s, d: ctx.enter_context(nc.sbuf_tensor(n, s, d))
        ps = lambda n, s: ctx.enter_context(nc.psum_tensor(n, s, F32))
        sem = lambda n: ctx.enter_context(nc.semaphore(n))
        k_stack = [sb(f"k_stack{i}", [S3 + 1, TP], F32R) for i in range(NS)]
        q_stack = [sb(f"q_stack{i}", [S3 + 1, GH * Q], F32R) for i in range(NS)]
        values = [sb(f"values{i}", [P, NT * HD], F32) for i in range(NS)]
        ones = sb("ones", [P, HD], F32)
        probs = [sb(f"probs{t}", [P, GH * Q], F32) for t in range(NT)]
        pair_sum = [sb(f"pair_sum{i}", [P, GH * Q], F32) for i in range(2)]
        part_max = sb("part_max", [P, UNITS, 2], F32)
        neg_max = sb("neg_max", [P, HD], F32R)
        neg_max_t = sb("neg_max_t", [P, HD], F32)
        context, denom = sb("context", [P, Q], F32), sb("denom", [P, Q], F32)
        recip, attn = sb("recip", [P, Q], F32), sb("attn", [P, Q], F32)
        attn_parts = sb("attn_parts", [P, 2, Q], F32R)
        first = ps("first", [P, NCH, BANK])
        second = [ps(f"second{i}", [P, BANK]) for i in range(2)]
        context_ps, denom_ps = ps("context_ps", [P, Q]), ps("denom_ps", [P, Q])

        consts_ready = sem("consts_ready")
        stacked = [sem(f"stacked{i}") for i in range(NS)]
        first_ready, first_read = sem("first_ready"), sem("first_read")
        neg_ready, neg_turned, neg_stacked = sem("neg_ready"), sem("neg_turned"), sem("neg_stacked")
        second_ready, exp_done = sem("second_ready"), sem("exp_done")
        context_done, denom_done = sem("context_done"), sem("denom_done")
        added = sem("added")
        context_copied, denom_copied = sem("context_copied"), sem("denom_copied")
        recip_done, attn_done, hi_done, lo_done = sem("recip_done"), sem("attn_done"), sem("a_hi_done"), sem("a_lo_done")
        attn_stored = sem("attn_stored")
        block = ctx.enter_context(nc.Block())

        LOADS = 7
        DENOM_TILE, DENOM_LAST = KP, KP + 1

        def exps(n, t):
            return n * TILES + (t + 1) * GH + 2

        def pairs_of(slot):
            return range(SHARE[slot], SHARE[slot + 1])

        @block.sync
        def _(sp):
            def load(n, s):
                kr = k_scr[bass.ds(n * HD, HD), :, :]
                qr = q_scr[bass.ds(n * P, P), :, :].rearrange("(h d) c q -> d c h q", d=HD)
                for r, part in enumerate((0, 0, 1)):
                    sp.dma_start(k_stack[s][r * HD:(r + 1) * HD, :].bitcast(F32), kr[:, part, :]).then_inc(stacked[s], 16)
                for r, part in enumerate((0, 1, 0)):
                    sp.dma_start(q_stack[s][r * HD:(r + 1) * HD, :].bitcast(F32).rearrange("d (h q) -> d h q", h=GH),
                                 qr[:, part]).then_inc(stacked[s], 16)

            def load_values(n, s):
                sp.dma_start(values[s][:, :], v_scr[bass.ds(n, 1), :, :].rearrange("o p f -> (o p) f")).then_inc(stacked[s], 16)

            def stack_max(n, s):
                sp.wait_ge(neg_turned, n + 1)
                row = q_stack[s][S3:S3 + 1, :].bitcast(F32).rearrange("o (u i c) -> o i u c", i=P // HD, c=HD)
                for i in range(P // HD):
                    sp.dma_start(row[:, i], neg_max_t[i * HD:i * HD + UNITS, :]).then_inc(neg_stacked, 16)

            def group(n, s):
                if not (isinstance(n, int) and n + 1 >= NG):
                    stack_max(n + 1, (s + 1) % NS)
                if not (isinstance(n, int) and n + NS >= NG):
                    sp.wait_ge(second_ready, (n + 1) * TILES)
                    load(n + NS, s)
                    sp.wait_ge(context_done, (n + 2) * NT)
                    load_values(n + NS, s)
                sp.wait_ge(lo_done, n + 2)
                sp.dma_start(a_scr[bass.ds(n, 1), :, :, :].rearrange("o p c q -> (o p) c q"),
                             attn_parts[:, :, :].bitcast(F32)).then_inc(attn_stored, 16)

            for n in range(NS):
                load(n, n)
                load_values(n, n)
            stack_max(0, 0)
            with sp.Fori(0, SP_LOOPS) as i:
                for s in range(BODY):
                    group(i * BODY + s, s)
            for n in range(SP_LOOPS * BODY, NG):
                group(n, n % NS)
            sp.wait_ge(attn_stored, (NG + 1) * 16)

        @block.gpsimd
        def _(pool):
            pool.sem_inc(added, KP)
            with pool.Fori(0, NG) as n:
                for k in range(KP):
                    pool.wait_ge(exp_done, exps(n, 2 * k + 1))
                    pool.wait_ge(denom_done, n * SB + (SB + k - 1 if k >= 2 else KP - 1 if k == 0 else DENOM_LAST))
                    nc.gpsimd.tensor_tensor(pair_sum[k % 2][:, :], probs[2 * k][:, :], probs[2 * k + 1][:, :],
                                            ALU.add).then_inc(added, 1)
                pool.wait_ge(hi_done, n + 1)
                nc.gpsimd.tensor_tensor(attn_parts[:, 1, :], attn[:, :], attn_parts[:, 0, :].bitcast(F32),
                                        ALU.subtract).then_inc(lo_done, 1)

        @block.scalar
        def _(act):
            act.sem_inc(exp_done, 2)

            def tile(n, t):
                rows = P if t < NT - 1 else TL
                act.wait_ge(context_done, n * NT + t + 1)
                if t < NT - 1:
                    act.wait_ge(added, n * KP + t // 2 + 1)
                else:
                    act.wait_ge(denom_done, n * SB + DENOM_TILE)
                for h in range(GH):
                    act.wait_ge(second_ready, n * TILES + t * GH + h + 1)
                    nc.scalar.activation(probs[t][0:rows, h * Q:(h + 1) * Q], second[h % 2][0:rows, :], ACT.Exp,
                                         scale=SCALE).then_inc(exp_done, 1)

            def copy_context(n):
                act.wait_ge(context_done, (n + 2) * NT)
                act.wait_ge(attn_done, n + 1)
                nc.scalar.activation(context[:, :], context_ps[:, :], ACT.Copy).then_inc(context_copied, 1)

            def copy_denom(n):
                act.wait_ge(denom_done, (n + 2) * SB)
                nc.scalar.activation(denom[:, :], denom_ps[:, :], ACT.Copy).then_inc(denom_copied, 1)

            tile(0, 0)
            tile(0, 1)
            with act.Fori(0, NG - 1) as n:
                for t in range(2, NT):
                    tile(n, t)
                tile(n + 1, 0)
                copy_context(n)
                tile(n + 1, 1)
                copy_denom(n)
            for t in range(2, NT):
                tile(NG - 1, t)
            copy_context(NG - 1)
            copy_denom(NG - 1)

        @block.vector
        def _(dve):
            dve.sem_inc(attn_done, 1)
            dve.sem_inc(lo_done, 1)
            dve.sem_inc(attn_stored, 16)
            nc.vector.memset(ones[:, :], 1.0).then_inc(consts_ready, 1)
            nc.vector.memset(neg_max[:, :].bitcast(F32), 0.0).then_inc(consts_ready, 1)
            for s in range(NS):
                nc.vector.memset(k_stack[s][S3:S3 + 1, :].bitcast(F32), 1.0).then_inc(consts_ready, 1)

            def read_pairs(n, slots):
                for slot in slots:
                    for q in pairs_of(slot):
                        dve.wait_ge(first_ready, n * PAIRS + q + 1)
                        half = q % 2
                        nc.vector.tensor_reduce(part_max[:, q // 2, half:half + 1], first[:, 2 * half:2 * half + 2, 0:CH],
                                                AX.XY, ALU.max).then_inc(first_read, 1)

            def finish_max(n):
                dve.wait_ge(first_read, (n + 1) * PAIRS)
                nc.vector.tensor_reduce(neg_max[:, 0:UNITS], part_max[:, :, :], AX.X, ALU.max,
                                        negate=True).then_inc(neg_ready, 1)
                dve.wait_ge(neg_ready, n + 1)
                if not (isinstance(n, int) and n == 0):
                    dve.wait_ge(neg_stacked, n * (P // HD) * 16)
                nc.vector.transpose(neg_max_t[:, :], neg_max[:, :].bitcast(F32)).then_inc(neg_turned, 1)

            def divide(n):
                dve.wait_ge(denom_copied, n + 1)
                nc.vector.reciprocal(recip[:, :], denom[:, :]).then_inc(recip_done, 1)
                dve.wait_ge(recip_done, n + 1)
                dve.wait_ge(context_copied, n + 1)
                dve.wait_ge(lo_done, n + 1)
                nc.vector.tensor_tensor(attn[:, :], context[:, :], recip[:, :], ALU.mult).then_inc(attn_done, 1)
                dve.wait_ge(attn_done, n + 2)
                dve.wait_ge(attn_stored, (n + 1) * 16)
                nc.vector.tensor_copy(attn_parts[:, 0, :], attn[:, :]).then_inc(hi_done, 1)

            dve.wait_ge(consts_ready, 2 + NS)
            read_pairs(0, range(NT))
            finish_max(0)
            read_pairs(1, range(2))
            with dve.Fori(0, NG - 2) as n:
                read_pairs(n + 1, range(2, NT))
                finish_max(n + 1)
                read_pairs(n + 2, range(2))
                divide(n)
            read_pairs(NG - 1, range(2, NT))
            finish_max(NG - 1)
            divide(NG - 2)
            divide(NG - 1)

        @block.tensor
        def _(pe):
            pe.sem_inc(context_done, NT)
            pe.sem_inc(denom_done, SB)

            def first_scores(n, s, slot, load=None):
                for q in pairs_of(slot):
                    u, half = divmod(q, 2)
                    if q == 0:
                        pe.wait_ge(stacked[s], load * (LOADS * 16))
                    if not (isinstance(n, int) and n * PAIRS + q < 2):
                        pe.wait_ge(first_read, n * PAIRS + q - 1)
                    for c in (2 * half, 2 * half + 1):
                        last = nc.tensor.matmul(first[:, c, 0:CH], q_stack[s][0:S3, u * P:(u + 1) * P],
                                                k_stack[s][0:S3, c * CH:(c + 1) * CH], start=True, stop=True)
                    last.then_inc(first_ready, 1)

            def second_scores(n, s, t, heads):
                rows = P if t < NT - 1 else TL
                for h in heads:
                    pe.wait_ge(exp_done, n * TILES + t * GH + h + 1)
                    nc.tensor.matmul(second[h % 2][0:rows, :], k_stack[s][:, t * P:t * P + rows],
                                     q_stack[s][:, h * Q:(h + 1) * Q], start=True, stop=True).then_inc(second_ready, 1)

            def context_tile(n, s, t):
                rows = P if t < NT - 1 else TL
                pe.wait_ge(exp_done, exps(n, t))
                if t == 0 and not (isinstance(n, int) and n == 0):
                    pe.wait_ge(context_copied, n)
                for h in range(GH):
                    last = nc.tensor.matmul(context_ps[h * HD:(h + 1) * HD, :], values[s][0:rows, t * HD:(t + 1) * HD],
                                            probs[t][0:rows, h * Q:(h + 1) * Q], start=t == 0, stop=t == NT - 1)
                last.then_inc(context_done, 1)

            def denom_product(source, rows, start, stop):
                for h in range(GH):
                    last = nc.tensor.matmul(denom_ps[h * HD:(h + 1) * HD, :], ones[0:rows, :],
                                            source[0:rows, h * Q:(h + 1) * Q], start=start, stop=stop)
                last.then_inc(denom_done, 1)

            def denom_pair(n, k):
                pe.wait_ge(added, n * KP + k + 1 + KP)
                if k == 0 and not (isinstance(n, int) and n == 0):
                    pe.wait_ge(denom_copied, n)
                denom_product(pair_sum[k % 2], P, k == 0, k == KP - 1)

            def stacked_max(n):
                pe.wait_ge(neg_stacked, (n + 1) * (P // HD) * 16)

            def group(i, s, more_first):
                n = i * BODY + s
                nxt, after = (s + 1) % NS, (s + 2) % NS
                for t in range(2, NT):
                    second_scores(n, s, t, (0, 1))
                    context_tile(n, s, t - 1)
                    second_scores(n, s, t, (2, 3))
                    if t >= 4 and t % 2 == 0:
                        denom_pair(n, t // 2 - 2)
                    if more_first >= 1:
                        first_scores(n + 1, nxt, t)
                if more_first >= 1:
                    stacked_max(n + 1)
                    second_scores(n + 1, nxt, 0, (0, 1))
                context_tile(n, s, NT - 1)
                if more_first >= 1:
                    second_scores(n + 1, nxt, 0, (2, 3))
                denom_product(probs[NT - 1], TL, False, False)
                if more_first >= 2:
                    first_scores(n + 2, after, 0, i + (s + 2) // NS + 1)
                if more_first >= 1:
                    second_scores(n + 1, nxt, 1, (0, 1))
                    context_tile(n + 1, nxt, 0)
                    second_scores(n + 1, nxt, 1, (2, 3))
                denom_pair(n, KP - 1)
                if more_first >= 2:
                    first_scores(n + 2, after, 1)

            pe.wait_ge(consts_ready, 2 + NS)
            for slot in range(NT):
                first_scores(0, 0, slot, 1)
            stacked_max(0)
            second_scores(0, 0, 0, range(GH))
            first_scores(1, 1, 0, 1)
            second_scores(0, 0, 1, (0, 1))
            context_tile(0, 0, 0)
            second_scores(0, 0, 1, (2, 3))
            first_scores(1, 1, 1)
            with pe.Fori(0, PE_LOOPS) as i:
                for s in range(BODY):
                    group(i, s, 2)
            for n in range(PE_LOOPS * BODY, NG):
                group(n // BODY, n % BODY, NG - 1 - n)


def output(nc, a_scr, wo, ao, bo, x, out):
    QT, NN = Q // P, H // BANK
    UN = QT * NN
    with ExitStack() as ctx:
        sb = lambda n, s, d: ctx.enter_context(nc.sbuf_tensor(n, s, d))
        sem = lambda n: ctx.enter_context(nc.semaphore(n))
        w_done = sem("wo_done")
        w, w_units, w_load, w_products, w_high, w_low = fold_weights(nc, ctx, "wo", H, [(ao, bo, wo, 0)], w_done)
        parts = [sb(f"a_parts{i}", [P, NKV, 2 * Q], F32R) for i in range(2)]
        res = sb("res", [P, QT, H], F32)
        banks = [ctx.enter_context(nc.psum_tensor(f"o_bank{i}", [P, BANK], F32)) for i in range(UN)]
        a_loaded = [sem(f"a_loaded{i}") for i in range(2)]
        x_loaded, o_ready, o_added, o_stored = sem("res_loaded"), sem("o_ready"), sem("o_added"), sem("o_stored")
        block = ctx.enter_context(nc.Block())

        @block.sync
        def _(sp):
            w_load(sp)
            with sp.Fori(0, B // 2) as bb:
                for half in range(2):
                    b = bb * 2 + half
                    sp.wait_ge(o_ready, (b + 1) * UN)
                    sp.dma_start(parts[half][:, :, :].bitcast(F32), a_scr[bass.ds(b * NKV, NKV), :, :, :].rearrange(
                        "g p c q -> p g (c q)")).then_inc(a_loaded[half], 16)

        @block.scalar
        def _(act):
            act.sem_inc(o_stored, 16)
            w_high(act)
            with act.Fori(0, B) as b:
                act.wait_ge(o_stored, (b + 1) * 16)
                act.dma_start(res[:, :, :], x[bass.ds(b, 1), :, :].rearrange(
                    "o (t p) n -> (o p) t n", p=P)).then_inc(x_loaded, 16)
                act.wait_ge(o_added, (b + 2) * UN)
                act.dma_start(out[bass.ds(b, 1), :, :].rearrange("o (t p) n -> (o p) t n", p=P),
                              res[:, :, :]).then_inc(o_stored, 16)
            act.wait_ge(o_stored, (B + 1) * 16)

        @block.vector
        def _(dve):
            dve.sem_inc(o_added, UN)
            w_low(dve, banks)
            with dve.Fori(0, B) as b:
                dve.wait_ge(x_loaded, (b + 1) * 16)
                for u in range(UN):
                    qt, nn = divmod(u, NN)
                    dve.wait_ge(o_ready, (b + 2) * UN + u + 1)
                    r = res[:, qt, nn * BANK:(nn + 1) * BANK]
                    nc.vector.tensor_tensor(r, banks[u][:, :], r, ALU.add).then_inc(o_added, 1)

        @block.tensor
        def _(pe):
            pe.sem_inc(o_ready, 2 * UN)
            w_products(pe, banks)
            pe.wait_ge(w_done, w_units)
            with pe.Fori(0, B // 2) as bb:
                for half in range(2):
                    b = bb * 2 + half
                    pe.wait_ge(a_loaded[half], (bb + 1) * 16)
                    for u in range(UN):
                        qt, nn = divmod(u, NN)
                        pe.wait_ge(o_added, b * UN + u + 1)
                        for i, (k, (wp, xp)) in enumerate((k, t) for k in range(KT) for t in TERMS):
                            q0 = xp * Q + qt * P
                            last = nc.tensor.matmul(banks[u][:, :], parts[half][:, k, q0:q0 + P],
                                                    w[:, wp, k, nn * BANK:(nn + 1) * BANK], start=i == 0,
                                                    stop=i == KT * len(TERMS) - 1)
                        last.then_inc(o_ready, 1)


def build(nc, xT, x, ctxT, wq, aq, bq, wk, ak, bk, wv, av, bv, wo, ao, bo, out):
    k_scr = nc.dram_tensor("k_scr", (B * KV, 2, TP), F32).ap()
    v_scr = nc.dram_tensor("v_scr", (NG, P, NT * HD), F32).ap()
    q_scr = nc.dram_tensor("q_scr", (B * H, 2, Q), F32).ap()
    a_scr = nc.dram_tensor("a_scr", (NG, P, 2, Q), F32).ap()
    keys_and_values(nc, ctxT, wk, ak, bk, wv, av, bv, k_scr, v_scr)
    queries(nc, xT, wq, aq, bq, q_scr)
    attention(nc, k_scr, v_scr, q_scr, a_scr)
    output(nc, a_scr, wo, ao, bo, x, out)


def kernel(**inputs):
    import concourse.bacc as bacc
    from concourse.bass_utils import run_bass_kernel_spmd

    g = {k.replace("L0_xattn_", ""): np.asarray(v) for k, v in inputs.items()}
    ctx = g["ctx_4096"]
    arrays = {
        "xT": g["x"].transpose(0, 2, 1),
        "x": g["x"],
        "ctxT": np.pad(ctx, ((0, 0), (0, TP - T), (0, 0)), mode="edge").transpose(0, 2, 1),
    }
    for s in "qkvo":
        arrays[f"W{s}"], arrays[f"A{s}T"], arrays[f"B{s}"] = g[f"W{s}"], g[f"A{s}"].T, g[f"B{s}"]
    arrays = {f"in_{k}": np.ascontiguousarray(v) for k, v in arrays.items()}
    nc = bacc.Bacc("TRN2", target_bir_lowering=False, num_devices=1)
    args = [nc.dram_tensor(k, v.shape, mybir.dt.from_np(v.dtype), kind="ExternalInput").ap() for k, v in arrays.items()]
    out = nc.dram_tensor("out", (B, Q, H), F32, kind="ExternalOutput").ap()
    build(nc, *args, out)
    return run_bass_kernel_spmd(nc, [arrays], core_ids=[0]).results[0]["out"]
```

```python
from contextlib import ExitStack

import numpy as np
import concourse.bass as bass
from concourse import mybir

F32 = mybir.dt.float32
F32R = mybir.dt.float32r
ALU = mybir.AluOpType
ACT = mybir.ActivationFunctionType
AX = mybir.AxisListType

B, Q, T, H = 4, 512, 1601, 1024
NH, NKV, R = 32, 8, 16
HD = H // NH
KV = NKV * HD
GH = NH // NKV
NG = B * NKV
LORA_SCALE = 2.0
P = 128
KT = H // P
NT = -(-T // P)
TP = NT * P
TL = T - (NT - 1) * P
BANK = 512
SCALE = float(HD) ** -0.5
TERMS = ((0, 0), (0, 1), (1, 0))


def fold_weights(nc, ctx, name, cols, pairs, done_sem):
    at = ctx.enter_context(nc.sbuf_tensor(f"{name}_at", [R, len(pairs), H], F32))
    lb = ctx.enter_context(nc.sbuf_tensor(f"{name}_lb", [R, cols], F32))
    raw = ctx.enter_context(nc.sbuf_tensor(f"{name}_raw", [P, KT, cols], F32))
    parts = ctx.enter_context(nc.sbuf_tensor(f"{name}_parts", [P, KT, 2, cols], F32R))
    lora_loaded = ctx.enter_context(nc.semaphore(f"{name}_lora_loaded"))
    tile_loaded = [ctx.enter_context(nc.semaphore(f"{name}_tile_loaded{k}")) for k in range(KT)]
    ab_ready = ctx.enter_context(nc.semaphore(f"{name}_ab_ready"))
    summed = ctx.enter_context(nc.semaphore(f"{name}_summed"))
    hi_done = ctx.enter_context(nc.semaphore(f"{name}_hi_done"))
    units = [(k, c) for k in range(KT) for c in range(0, cols, BANK)]

    def load(sp):
        for j, (a, b, w, c0) in enumerate(pairs):
            sp.dma_start(at[:, j, :], a).then_inc(lora_loaded, 16)
            sp.dma_start(lb[:, c0:c0 + b.shape[1]], b).then_inc(lora_loaded, 16)
        for k in range(KT):
            for a, b, w, c0 in pairs:
                sp.dma_start(raw[:, k, c0:c0 + b.shape[1]], w[k * P:(k + 1) * P, :]).then_inc(tile_loaded[k], 16)

    def products(pe, banks):
        pe.wait_ge(lora_loaded, 32 * len(pairs))
        for u, (k, c) in enumerate(units):
            if u >= len(banks):
                pe.wait_ge(summed, u - len(banks) + 1)
            for j, (_, b, _, c0) in enumerate(pairs):
                lo, hi = max(c, c0), min(c + BANK, c0 + b.shape[1])
                if lo < hi:
                    last = nc.tensor.matmul(banks[u % len(banks)][:, lo - c:hi - c], at[:, j, k * P:(k + 1) * P],
                                            lb[:, lo:hi], start=True, stop=True)
            last.then_inc(ab_ready, 1)

    def high_parts(act):
        for u, (k, c) in enumerate(units):
            act.wait_ge(summed, u + 1)
            nc.scalar.activation(parts[:, k, 0, c:c + BANK], raw[:, k, c:c + BANK], ACT.Copy).then_inc(hi_done, 1)

    def sums_and_low_parts(dve, banks):
        def low(u):
            k, c = units[u]
            dve.wait_ge(hi_done, u + 1)
            nc.vector.tensor_tensor(parts[:, k, 1, c:c + BANK], raw[:, k, c:c + BANK],
                                    parts[:, k, 0, c:c + BANK].bitcast(F32), ALU.subtract).then_inc(done_sem, 1)

        for u, (k, c) in enumerate(units):
            dve.wait_ge(tile_loaded[k], 16 * len(pairs))
            dve.wait_ge(ab_ready, u + 1)
            nc.vector.scalar_tensor_tensor(out=raw[:, k, c:c + BANK], in0=banks[u % len(banks)][:, :],
                                           scalar=LORA_SCALE, in1=raw[:, k, c:c + BANK],
                                           op0=ALU.mult, op1=ALU.add).then_inc(summed, 1)
            if u >= 1:
                low(u - 1)
        low(len(units) - 1)

    return parts, len(units), load, products, high_parts, sums_and_low_parts


def keys_and_values(nc, ctxT, wk, ak, bk, wv, av, bv, k_scr, v_scr):
    NC = -(-TP // BANK)
    assert NC % 2 == 0
    ends = [-(-NT * (c + 1) // NC) for c in range(NC)]
    starts = [0] + ends[:-1]
    widths = [(e - a) * P for a, e in zip(starts, ends)]
    MK = KV // P
    with ExitStack() as ctx:
        sb = lambda n, s, d: ctx.enter_context(nc.sbuf_tensor(n, s, d))
        sem = lambda n: ctx.enter_context(nc.semaphore(n))
        w_done = sem("wkv_done")
        w, w_units, w_load, w_products, w_high, w_low = fold_weights(
            nc, ctx, "wkv", 2 * KV, [(ak, bk, wk, 0), (av, bv, wv, KV)], w_done)
        raw = [sb(f"ctx_raw{i}", [P, KT, BANK], F32) for i in range(2)]
        parts = [sb(f"ctx_parts{i}", [P, 2, KT, BANK], F32R) for i in range(2)]
        k_out = [sb(f"k_out{i}", [P, 2, BANK], F32R) for i in range(MK)]
        v_out = sb("v_out", [P, NKV, NT, HD], F32)
        banks = [ctx.enter_context(nc.psum_tensor(f"kv_bank{i}", [P, BANK], F32)) for i in range(8)]
        k_bank, v_bank = banks[0:4], banks[4:8]
        ctx_loaded = [sem(f"ctx_loaded{i}") for i in range(2)]
        ctx_hi, ctx_lo = sem("ctx_hi"), sem("ctx_lo")
        k_ready, k_hi, k_lo = sem("k_ready"), sem("k_hi"), sem("k_lo")
        v_ready, v_hi, v_copied = sem("v_ready"), sem("v_hi"), sem("v_copied")
        k_stored, v_stored = [sem(f"k_stored{i}") for i in range(MK)], sem("v_stored")
        block = ctx.enter_context(nc.Block())

        def by_head(columns):
            return columns.rearrange("p (g d) -> p g d", g=NKV)

        def v_tiles_before(b, c):
            return b * NT + (ends[c - 2] + NT if c >= 2 else ends[c - 2])

        @block.sync
        def _(sp):
            def load(b, c):
                sp.wait_ge(ctx_lo, b * NC + c - 1 + NC)
                sp.dma_start(raw[c % 2][:, :, 0:widths[c]],
                             ctxT[bass.ds(b, 1), :, starts[c] * P:ends[c] * P].rearrange(
                                 "o (k p) t -> (o p) k t", p=P)).then_inc(ctx_loaded[c % 2], 16)

            def batch(b, last):
                for c in range(NC):
                    if c + 1 < NC:
                        load(b, c + 1)
                    elif not last:
                        load(b + 1, 0)
                    for m in range(MK):
                        sp.wait_ge(k_lo, b * (NC * MK) + c * MK + m + 1 + 4)
                        sp.dma_start(k_scr[bass.ds(b * KV + m * P, P), :, starts[c] * P:ends[c] * P],
                                     k_out[m][:, :, 0:widths[c]].bitcast(F32)).then_inc(k_stored[m], 16)
                sp.wait_ge(v_copied, (b + 2) * NT)
                sp.dma_start(v_scr[bass.ds(b * NKV, NKV), :, :].rearrange("g p f -> p g f"),
                             v_out[:, :, :, :].rearrange("p g t d -> p g (t d)")).then_inc(v_stored, 16)

            w_load(sp)
            load(0, 0)
            with sp.Fori(0, B - 1) as b:
                batch(b, False)
            batch(B - 1, True)
            for m in range(MK):
                sp.wait_ge(k_stored[m], (B * NC + 1) * 16)
            sp.wait_ge(v_stored, (B + 1) * 16)

        @block.scalar
        def _(act):
            def split(b, c):
                n = widths[c]
                act.wait_ge(ctx_loaded[c % 2], (b * (NC // 2) + c // 2 + 1) * 16)
                act.wait_ge(v_ready, v_tiles_before(b, c))
                nc.scalar.activation(parts[c % 2][:, 0, :, 0:n], raw[c % 2][:, :, 0:n], ACT.Copy).then_inc(ctx_hi, 1)

            def batch(b, last):
                for c in range(NC):
                    n = widths[c]
                    for m in range(MK):
                        u = b * (NC * MK) + c * MK + m
                        act.wait_ge(k_ready, u + 1)
                        act.wait_ge(k_stored[m], (b * NC + c + 1) * 16)
                        nc.scalar.activation(k_out[m][:, 0, 0:n], k_bank[(c * MK + m) % 4][:, 0:n],
                                             ACT.Copy).then_inc(k_hi, 1)
                    if c + 1 < NC:
                        split(b, c + 1)
                    elif not last:
                        split(b + 1, 0)
                    for t in range(starts[c], ends[c]):
                        act.wait_ge(v_ready, b * NT + t + 1 + NT)
                        if t == 0:
                            act.wait_ge(v_stored, (b + 1) * 16)
                        nc.scalar.activation(v_out[:, :, t, :], by_head(v_bank[t % 4][:, 0:KV]),
                                             ACT.Copy).then_inc(v_hi, 1)

            act.sem_inc(v_stored, 16)
            for m in range(MK):
                act.sem_inc(k_stored[m], 16)
            w_high(act)
            split(0, 0)
            with act.Fori(0, B - 1) as b:
                batch(b, False)
            batch(B - 1, True)

        @block.vector
        def _(dve):
            def split(b, c):
                n = widths[c]
                dve.wait_ge(ctx_hi, b * NC + c + 1)
                nc.vector.tensor_tensor(parts[c % 2][:, 1, :, 0:n], raw[c % 2][:, :, 0:n],
                                        parts[c % 2][:, 0, :, 0:n].bitcast(F32), ALU.subtract).then_inc(ctx_lo, 1)

            def batch(b, last):
                for c in range(NC):
                    n = widths[c]
                    for m in range(MK):
                        u = b * (NC * MK) + c * MK + m
                        dve.wait_ge(k_hi, u + 1)
                        nc.vector.tensor_tensor(k_out[m][:, 1, 0:n], k_bank[(c * MK + m) % 4][:, 0:n],
                                                k_out[m][:, 0, 0:n].bitcast(F32), ALU.subtract).then_inc(k_lo, 1)
                    if c + 1 < NC:
                        split(b, c + 1)
                    elif not last:
                        split(b + 1, 0)
                    for t in range(starts[c], ends[c]):
                        dve.wait_ge(v_hi, b * NT + t + 1)
                        nc.vector.tensor_tensor(v_out[:, :, t, :], by_head(v_bank[t % 4][:, KV:2 * KV]),
                                                v_out[:, :, t, :], ALU.add).then_inc(v_copied, 1)

            dve.sem_inc(v_copied, NT)
            dve.sem_inc(ctx_lo, NC)
            dve.sem_inc(k_lo, 4)
            w_low(dve, banks)
            split(0, 0)
            with dve.Fori(0, B - 1) as b:
                batch(b, False)
            batch(B - 1, True)

        @block.tensor
        def _(pe):
            pe.sem_inc(v_ready, NT)
            w_products(pe, banks)
            pe.wait_ge(w_done, w_units)
            with pe.Fori(0, B) as b:
                for c in range(NC):
                    n = widths[c]
                    x = parts[c % 2]
                    pe.wait_ge(ctx_lo, b * NC + c + 1 + NC)
                    for m in range(MK):
                        u = b * (NC * MK) + c * MK + m
                        pe.wait_ge(k_lo, u + 1)
                        for i, (k, (wp, xp)) in enumerate((k, t) for k in range(KT) for t in TERMS):
                            last = nc.tensor.matmul(k_bank[(c * MK + m) % 4][:, 0:n], w[:, k, wp, m * P:(m + 1) * P],
                                                    x[:, xp, k, 0:n], start=i == 0, stop=i == KT * len(TERMS) - 1)
                        last.then_inc(k_ready, 1)
                    for t in range(starts[c], ends[c]):
                        t0 = (t - starts[c]) * P
                        used = t - 4 + NT if t >= 4 else (NT - 1 - (NT - 1 - t) % 4)
                        pe.wait_ge(v_copied, b * NT + used + 1)
                        for k in range(KT):
                            nc.tensor.matmul(v_bank[t % 4][:, :], x[:, 0, k, t0:t0 + P], w[:, k, :, KV:2 * KV],
                                             start=k == 0, stop=k == KT - 1)
                            last = nc.tensor.matmul(v_bank[t % 4][:, 0:KV], x[:, 1, k, t0:t0 + P],
                                                    w[:, k, 0, KV:2 * KV], start=False, stop=k == KT - 1,
                                                    skip_group_check=True)
                        last.then_inc(v_ready, 1)


def queries(nc, xT, wq, aq, bq, q_scr):
    MQ = H // P
    with ExitStack() as ctx:
        sb = lambda n, s, d: ctx.enter_context(nc.sbuf_tensor(n, s, d))
        sem = lambda n: ctx.enter_context(nc.semaphore(n))
        w_done = sem("wq_done")
        w, w_units, w_load, w_products, w_high, w_low = fold_weights(nc, ctx, "wq", H, [(aq, bq, wq, 0)], w_done)
        raw = sb("x_raw", [P, KT, Q], F32)
        parts = [sb(f"x_parts{i}", [P, 2, KT, Q], F32R) for i in range(2)]
        q_out = [sb(f"q_out{i}", [P, 2, Q], F32R) for i in range(2)]
        banks = [ctx.enter_context(nc.psum_tensor(f"q_bank{i}", [P, Q], F32)) for i in range(MQ)]
        x_loaded, x_hi, x_lo = sem("x_loaded"), sem("x_hi"), sem("x_lo")
        q_ready, q_hi, q_lo = sem("q_ready"), sem("q_hi"), sem("q_lo")
        q_stored = [sem(f"q_stored{i}") for i in range(2)]
        block = ctx.enter_context(nc.Block())

        def evacuations(bb, half):
            return [((bb * 2 + half) * MQ + m, m, m % 2, (bb * 2 + half) * (MQ // 2) + m // 2) for m in range(MQ)]

        @block.sync
        def _(sp):
            def load(b):
                if not (isinstance(b, int) and b == 0):
                    sp.wait_ge(x_lo, b)
                sp.dma_start(raw[:, :, :], xT[bass.ds(b, 1), :, :].rearrange(
                    "o (k p) t -> (o p) k t", p=P)).then_inc(x_loaded, 16)

            def batch(b, more):
                if more:
                    load(b + 2)
                for m in range(MQ):
                    sp.wait_ge(q_lo, b * MQ + m + 1 + MQ)
                    sp.dma_start(q_scr[bass.ds(b * H + m * P, P), :, :],
                                 q_out[m % 2][:, :, :].bitcast(F32)).then_inc(q_stored[m % 2], 16)

            w_load(sp)
            load(0)
            load(1)
            with sp.Fori(0, B - 2) as b:
                batch(b, True)
            batch(B - 2, False)
            batch(B - 1, False)
            for s in range(2):
                sp.wait_ge(q_stored[s], (B * (MQ // 2) + 1) * 16)

        @block.scalar
        def _(act):
            for s in range(2):
                act.sem_inc(q_stored[s], 16)
            w_high(act)

            def split(bb, half):
                act.wait_ge(x_loaded, (bb * 2 + half + 1) * 16)
                act.wait_ge(q_ready, (bb * 2 + half + 1) * MQ)
                nc.scalar.activation(parts[half][:, 0], raw[:, :, :], ACT.Copy).then_inc(x_hi, 1)

            def batch(bb, half):
                for u, m, s, stores in evacuations(bb, half):
                    act.wait_ge(q_ready, u + 1 + 2 * MQ)
                    act.wait_ge(q_stored[s], (stores + 1) * 16)
                    nc.scalar.activation(q_out[s][:, 0, :], banks[m][:, :], ACT.Copy).then_inc(q_hi, 1)

            split(0, 0)
            with act.Fori(0, B // 2 - 1) as bb:
                split(bb, 1)
                batch(bb, 0)
                split(bb + 1, 0)
                batch(bb, 1)
            split(B // 2 - 1, 1)
            batch(B // 2 - 1, 0)
            batch(B // 2 - 1, 1)

        @block.vector
        def _(dve):
            dve.sem_inc(q_lo, MQ)
            w_low(dve, banks)

            def split(bb, half):
                dve.wait_ge(x_hi, bb * 2 + half + 1)
                nc.vector.tensor_tensor(parts[half][:, 1], raw[:, :, :], parts[half][:, 0].bitcast(F32),
                                        ALU.subtract).then_inc(x_lo, 1)

            def batch(bb, half):
                for u, m, s, _ in evacuations(bb, half):
                    dve.wait_ge(q_hi, u + 1)
                    nc.vector.tensor_tensor(q_out[s][:, 1, :], banks[m][:, :], q_out[s][:, 0, :].bitcast(F32),
                                            ALU.subtract).then_inc(q_lo, 1)

            split(0, 0)
            with dve.Fori(0, B // 2 - 1) as bb:
                split(bb, 1)
                batch(bb, 0)
                split(bb + 1, 0)
                batch(bb, 1)
            split(B // 2 - 1, 1)
            batch(B // 2 - 1, 0)
            batch(B // 2 - 1, 1)

        @block.tensor
        def _(pe):
            pe.sem_inc(q_ready, 2 * MQ)
            w_products(pe, banks)
            pe.wait_ge(w_done, w_units)
            with pe.Fori(0, B // 2) as bb:
                for half in range(2):
                    pe.wait_ge(x_lo, bb * 2 + half + 1)
                    for u, m, _, _ in evacuations(bb, half):
                        pe.wait_ge(q_lo, u + 1)
                        for i, (k, (wp, xp)) in enumerate((k, t) for k in range(KT) for t in TERMS):
                            last = nc.tensor.matmul(banks[m][:, :], w[:, k, wp, m * P:(m + 1) * P],
                                                    parts[half][:, xp, k, :], start=i == 0,
                                                    stop=i == KT * len(TERMS) - 1)
                        last.then_inc(q_ready, 1)


def attention(nc, k_scr, v_scr, q_scr, a_scr):
    S3 = 3 * HD
    QT = Q // P
    UNITS = GH * QT
    CH = 402
    NCH = 4
    assert CH % 2 == 0 and T <= NCH * CH <= TP
    PAIRS = UNITS * NCH // 2
    NS = 3
    HEAD = 5
    ORDER = ["DPCP01P23P"] + ["0P1CP2P3D"] * (HEAD - 1) + ["0P1C23P"] * 6 + ["0N1C23N"] * 2
    EARLY = sum(o.count("N") for o in ORDER)
    BEFORE = [EARLY + sum(o.count("P") for o in ORDER[:t]) for t in range(NT + 1)]
    assert len(ORDER) == NT and BEFORE[NT] == PAIRS
    assert not any("N" in o and "P" in "".join(ORDER[t:]) for t, o in enumerate(ORDER))
    EARLY_BEFORE = [sum(o.count("N") for o in ORDER[:t]) for t in range(NT + 1)]
    TURN = max(t for t, o in enumerate(ORDER) if "P" in o)
    RECIP_SLOTS = range(NT - 8, NT)
    RECIPS = len(RECIP_SLOTS)
    BANK_OF = [j % 2 if j < HEAD * GH else (j - HEAD * GH) % 3 for j in range(GH * NT)]
    RUNS = ((0, 1, 2, 3), (4, 5, 6, 7), (8, 9, 10))
    ADDS = sum(len(r) - 1 for r in RUNS)
    ADDED_AT = {t: sum(len(x) - 1 for x in RUNS[:j]) + max(i, 1) for j, r in enumerate(RUNS) for i, t in enumerate(r)}
    BLOCKS = (("run", 0, NT), ("run", 1, NT + 1), ("tile", 11, NT + 2), ("tile", 12, NT + 3), ("run", 2, NT + 4))
    BLOCK_OF = {(kind, x): i + 1 for i, (kind, x, _) in enumerate(BLOCKS)}
    TILES = GH * NT
    SB = len(BLOCKS)
    BODY = 3
    assert all("D" in ORDER[at % NT] for _, _, at in BLOCKS)
    assert all(t in ADDED_AT or ("tile", t) in BLOCK_OF for t in range(NT))
    PE_LOOPS = (NG - 2) // BODY
    SP_LOOPS = (NG - NS) // BODY

    with ExitStack() as ctx:
        sb = lambda n, s, d: ctx.enter_context(nc.sbuf_tensor(n, s, d))
        ps = lambda n, s: ctx.enter_context(nc.psum_tensor(n, s, F32))
        sem = lambda n: ctx.enter_context(nc.semaphore(n))
        k_stack = [sb(f"k_stack{i}", [S3 + 1, TP], F32R) for i in range(NS)]
        q_stack = [sb(f"q_stack{i}", [S3 + 1, GH * Q], F32R) for i in range(NS)]
        values = [sb(f"values{i}", [P, NT * HD], F32) for i in range(NS)]
        ones = sb("ones", [P, HD], F32)
        probs = [sb(f"probs{t}", [P, GH * Q], F32) for t in range(NT)]
        run_sum = [sb(f"run_sum{i}", [P, GH * Q], F32) for i in range(len(RUNS))]
        part_max = sb("part_max", [P, UNITS, 2], F32)
        neg_max = sb("neg_max", [P, HD], F32R)
        neg_max_t = sb("neg_max_t", [P, HD], F32)
        context, denom = sb("context", [P, Q], F32), sb("denom", [P, Q], F32)
        recip, attn = sb("recip", [P, Q], F32), sb("attn", [P, Q], F32)
        attn_parts = sb("attn_parts", [P, 2, Q], F32R)
        first = ps("first", [P, NCH, BANK])
        second = [ps(f"second{i}", [P, BANK]) for i in range(3)]
        context_ps, denom_ps = ps("context_ps", [P, Q]), second[2]

        consts_ready = sem("consts_ready")
        stacked = [sem(f"stacked{i}") for i in range(NS)]
        first_ready, first_read = sem("first_ready"), sem("first_read")
        neg_ready, neg_turned, neg_stacked = sem("neg_ready"), sem("neg_turned"), sem("neg_stacked")
        second_ready, exp_done = sem("second_ready"), sem("exp_done")
        context_done, denom_done = sem("context_done"), sem("denom_done")
        added = sem("added")
        context_copied, denom_copied = sem("context_copied"), sem("denom_copied")
        recip_done, attn_done, hi_done, lo_done = sem("recip_done"), sem("attn_done"), sem("a_hi_done"), sem("a_lo_done")
        attn_stored = sem("attn_stored")
        block = ctx.enter_context(nc.Block())

        LOADS = 7

        def exps(n, t):
            return n * TILES + (t + 1) * GH + 2

        @block.sync
        def _(sp):
            def load(n, s):
                kr = k_scr[bass.ds(n * HD, HD), :, :]
                qr = q_scr[bass.ds(n * P, P), :, :].rearrange("(h d) c q -> d c h q", d=HD)
                for r, part in enumerate((0, 0, 1)):
                    sp.dma_start(k_stack[s][r * HD:(r + 1) * HD, :].bitcast(F32), kr[:, part, :]).then_inc(stacked[s], 16)
                for r, part in enumerate((0, 1, 0)):
                    sp.dma_start(q_stack[s][r * HD:(r + 1) * HD, :].bitcast(F32).rearrange("d (h q) -> d h q", h=GH),
                                 qr[:, part]).then_inc(stacked[s], 16)

            def load_values(n, s):
                sp.dma_start(values[s][:, :], v_scr[bass.ds(n, 1), :, :].rearrange("o p f -> (o p) f")).then_inc(stacked[s], 16)

            def stack_max(n, s):
                sp.wait_ge(neg_turned, n + 1)
                row = q_stack[s][S3:S3 + 1, :].bitcast(F32).rearrange("o (u i c) -> o i u c", i=P // HD, c=HD)
                for i in range(P // HD):
                    sp.dma_start(row[:, i], neg_max_t[i * HD:i * HD + UNITS, :]).then_inc(neg_stacked, 16)

            def store(n):
                sp.wait_ge(lo_done, n + 2)
                sp.dma_start(a_scr[bass.ds(n, 1), :, :, :].rearrange("o p c q -> (o p) c q"),
                             attn_parts[:, :, :].bitcast(F32)).then_inc(attn_stored, 16)

            def group(n, s):
                known = isinstance(n, int)
                if not (known and n + 1 >= NG):
                    stack_max(n + 1, (s + 1) % NS)
                if not (known and n + NS >= NG):
                    sp.wait_ge(second_ready, (n + 1) * TILES)
                    load(n + NS, s)
                    sp.wait_ge(context_done, (n + 2) * NT)
                    load_values(n + NS, s)
                if not (known and n == 0):
                    store(n - 1)

            for n in range(NS):
                load(n, n)
                load_values(n, n)
            stack_max(0, 0)
            for n in range(BODY):
                group(n, n)
            with sp.Fori(1, SP_LOOPS) as i:
                for s in range(BODY):
                    group(i * BODY + s, s)
            for n in range(SP_LOOPS * BODY, NG):
                group(n, n % NS)
            store(NG - 1)
            sp.wait_ge(attn_stored, (NG + 1) * 16)

        @block.gpsimd
        def _(pool):
            def add_runs(n):
                count = 0
                for j, run in enumerate(RUNS):
                    pool.wait_ge(denom_done, n * SB + BLOCK_OF["run", j])
                    for i in range(1, len(run)):
                        pool.wait_ge(exp_done, exps(n, run[i]))
                        if i > 1:
                            pool.wait_ge(added, (n + 1) * ADDS + count)
                        nc.gpsimd.tensor_tensor(run_sum[j][:, :], (probs[run[0]] if i == 1 else run_sum[j])[:, :],
                                                probs[run[i]][:, :], ALU.add).then_inc(added, 1)
                        count += 1

            def low_part(n):
                pool.wait_ge(hi_done, n + 1)
                nc.gpsimd.tensor_tensor(attn_parts[:, 1, :], attn[:, :], attn_parts[:, 0, :].bitcast(F32),
                                        ALU.subtract).then_inc(lo_done, 1)

            pool.sem_inc(added, ADDS)
            add_runs(0)
            with pool.Fori(1, NG) as n:
                add_runs(n)
                low_part(n - 1)
            low_part(NG - 1)

        @block.scalar
        def _(act):
            act.sem_inc(exp_done, 2)

            def tile(n, t):
                rows = P if t < NT - 1 else TL
                act.wait_ge(context_done, n * NT + t + 1)
                if t in ADDED_AT:
                    act.wait_ge(added, n * ADDS + ADDED_AT[t])
                else:
                    act.wait_ge(denom_done, n * SB + BLOCK_OF["tile", t])
                for h in range(GH):
                    act.wait_ge(second_ready, n * TILES + t * GH + h + 1)
                    nc.scalar.activation(probs[t][0:rows, h * Q:(h + 1) * Q], second[BANK_OF[t * GH + h]][0:rows, :],
                                         ACT.Exp, scale=SCALE).then_inc(exp_done, 1)

            def copy_context(n):
                act.wait_ge(context_done, (n + 2) * NT)
                act.wait_ge(attn_done, n + 1)
                nc.scalar.activation(context[:, :], context_ps[:, :], ACT.Copy).then_inc(context_copied, 1)

            def copy_denom(n):
                act.wait_ge(denom_done, (n + 2) * SB)
                nc.scalar.activation(denom[:, :], denom_ps[:, :], ACT.Copy).then_inc(denom_copied, 1)

            for t in range(HEAD):
                tile(0, t)
            with act.Fori(0, NG - 1) as n:
                for t in range(HEAD, NT):
                    tile(n, t)
                copy_context(n)
                for t in range(HEAD):
                    tile(n + 1, t)
                copy_denom(n)
            for t in range(HEAD, NT):
                tile(NG - 1, t)
            copy_context(NG - 1)
            copy_denom(NG - 1)

        @block.vector
        def _(dve):
            dve.sem_inc(attn_done, 1)
            dve.sem_inc(lo_done, 1)
            dve.sem_inc(attn_stored, 16)
            nc.vector.memset(ones[:, :], 1.0).then_inc(consts_ready, 1)
            nc.vector.memset(neg_max[:, :].bitcast(F32), 0.0).then_inc(consts_ready, 1)
            for s in range(NS):
                nc.vector.memset(k_stack[s][S3:S3 + 1, :].bitcast(F32), 1.0).then_inc(consts_ready, 1)

            def read_pairs(n, pairs):
                for q in pairs:
                    dve.wait_ge(first_ready, n * PAIRS + q + 1)
                    half = q % 2
                    nc.vector.tensor_reduce(part_max[:, q // 2, half:half + 1], first[:, 2 * half:2 * half + 2, 0:CH],
                                            AX.XY, ALU.max).then_inc(first_read, 1)

            def finish_max(n):
                dve.wait_ge(first_read, (n + 1) * PAIRS)
                nc.vector.tensor_reduce(neg_max[:, 0:UNITS], part_max[:, :, :], AX.X, ALU.max,
                                        negate=True).then_inc(neg_ready, 1)
                dve.wait_ge(neg_ready, n + 1)
                if not (isinstance(n, int) and n == 0):
                    dve.wait_ge(neg_stacked, n * (P // HD) * 16)
                nc.vector.transpose(neg_max_t[:, :], neg_max[:, :].bitcast(F32)).then_inc(neg_turned, 1)

            def reciprocals(n, part):
                cols = slice(part * Q // RECIPS, (part + 1) * Q // RECIPS)
                dve.wait_ge(denom_copied, n + 1)
                nc.vector.reciprocal(recip[:, cols], denom[:, cols]).then_inc(recip_done, 1)

            def divide(n):
                dve.wait_ge(recip_done, (n + 1) * RECIPS)
                dve.wait_ge(context_copied, n + 1)
                dve.wait_ge(lo_done, n + 1)
                nc.vector.tensor_tensor(attn[:, :], context[:, :], recip[:, :], ALU.mult).then_inc(attn_done, 1)

            def high_part(n):
                dve.wait_ge(attn_done, n + 2)
                dve.wait_ge(attn_stored, (n + 1) * 16)
                nc.vector.tensor_copy(attn_parts[:, 0, :], attn[:, :]).then_inc(hi_done, 1)

            def middle(n, divided=True, more=True):
                for t in range(HEAD, NT):
                    read_pairs(n + 1, range(BEFORE[t], BEFORE[t + 1]))
                    if t == TURN:
                        finish_max(n + 1)
                    if more:
                        read_pairs(n + 2, range(EARLY_BEFORE[t], EARLY_BEFORE[t + 1]))
                    if divided and t in RECIP_SLOTS:
                        reciprocals(n - 1, RECIP_SLOTS.index(t))
                if divided:
                    divide(n - 1)
                if more:
                    read_pairs(n + 2, range(EARLY, BEFORE[1]))
                if divided:
                    high_part(n - 1)
                if more:
                    read_pairs(n + 2, range(BEFORE[1], BEFORE[HEAD]))

            dve.wait_ge(consts_ready, 2 + NS)
            read_pairs(0, range(PAIRS))
            finish_max(0)
            read_pairs(1, range(BEFORE[HEAD]))
            middle(0, divided=False)
            with dve.Fori(1, NG - 2) as n:
                middle(n)
            middle(NG - 2, more=False)
            for n in (NG - 2, NG - 1):
                for part in range(RECIPS):
                    reciprocals(n, part)
                divide(n)
                high_part(n)

        @block.tensor
        def _(pe):
            pe.sem_inc(context_done, NT)
            pe.sem_inc(denom_done, SB)

            def first_scores(n, s, q, load=None):
                u, half = divmod(q, 2)
                if q == 0:
                    pe.wait_ge(stacked[s], load * (LOADS * 16))
                if not (isinstance(n, int) and n * PAIRS + q < 2):
                    pe.wait_ge(first_read, n * PAIRS + q - 1)
                for c in (2 * half, 2 * half + 1):
                    last = nc.tensor.matmul(first[:, c, 0:CH], q_stack[s][0:S3, u * P:(u + 1) * P],
                                            k_stack[s][0:S3, c * CH:(c + 1) * CH], start=True, stop=True)
                last.then_inc(first_ready, 1)

            def second_scores(n, s, t, h):
                rows = P if t < NT - 1 else TL
                if t == 0 and h == 0:
                    pe.wait_ge(neg_stacked, (n + 1) * (P // HD) * 16)
                j = t * GH + h
                if j > HEAD * GH and BANK_OF[j] == 2 and 2 not in BANK_OF[HEAD * GH:j]:
                    if not (isinstance(n, int) and n == 0):
                        pe.wait_ge(denom_copied, n)
                else:
                    user = max(i for i in range(-2, j) if BANK_OF[i] == BANK_OF[j])
                    pe.wait_ge(exp_done, n * TILES + user + 1 + 2)
                nc.tensor.matmul(second[BANK_OF[j]][0:rows, :], k_stack[s][:, t * P:t * P + rows],
                                 q_stack[s][:, h * Q:(h + 1) * Q], start=True, stop=True).then_inc(second_ready, 1)

            def context_tile(n, s, t):
                rows = P if t < NT - 1 else TL
                pe.wait_ge(exp_done, exps(n, t))
                if t == 0 and not (isinstance(n, int) and n == 0):
                    pe.wait_ge(context_copied, n)
                for h in range(GH):
                    last = nc.tensor.matmul(context_ps[h * HD:(h + 1) * HD, :], values[s][0:rows, t * HD:(t + 1) * HD],
                                            probs[t][0:rows, h * Q:(h + 1) * Q], start=t == 0, stop=t == NT - 1)
                last.then_inc(context_done, 1)

            def denominators(n, i):
                kind, x, _ = BLOCKS[i]
                if kind == "run":
                    source, rows = run_sum[x], P
                    pe.wait_ge(added, (n + 1) * ADDS + ADDED_AT[RUNS[x][-1]])
                else:
                    source, rows = probs[x], P if x < NT - 1 else TL
                    pe.wait_ge(exp_done, exps(n, x))
                if i == 0:
                    user = max(j for j in range(TILES) if BANK_OF[j] == 2)
                    pe.wait_ge(exp_done, n * TILES + user + 1 + 2)
                for h in range(GH):
                    last = nc.tensor.matmul(denom_ps[h * HD:(h + 1) * HD, :], ones[0:rows, :],
                                            source[0:rows, h * Q:(h + 1) * Q], start=i == 0, stop=i == SB - 1)
                last.then_inc(denom_done, 1)

            def slot(n, s, t, before=None, ahead=True, load=None, early=True):
                q = BEFORE[t]
                e = EARLY_BEFORE[t]
                for step in ORDER[t]:
                    if step == "P":
                        if ahead:
                            first_scores(n + 1, (s + 1) % NS, q, load)
                        q += 1
                    elif step == "N":
                        if early:
                            first_scores(n + 2, (s + 2) % NS, e, load)
                        e += 1
                    elif step == "C":
                        if t >= 1:
                            context_tile(n, s, t - 1)
                        elif before is not None:
                            context_tile(before, (s - 1) % NS, NT - 1)
                    elif step == "D":
                        for i, (_, _, at) in enumerate(BLOCKS):
                            if at == t:
                                denominators(n, i)
                            elif at == t + NT and before is not None:
                                denominators(before, i)
                    else:
                        second_scores(n, s, t, int(step))

            def group(i, s, ahead):
                n = i * BODY + s
                for t in range(HEAD, NT):
                    slot(n, s, t, ahead=ahead >= 1, load=i + (s + 2) // NS + 1, early=ahead >= 2)
                if ahead >= 1:
                    for t in range(HEAD):
                        slot(n + 1, (s + 1) % NS, t, before=n, ahead=ahead >= 2, load=i + (s + 2) // NS + 1)
                else:
                    context_tile(n, s, NT - 1)
                    for j, (_, _, at) in enumerate(BLOCKS):
                        if at >= NT:
                            denominators(n, j)

            pe.wait_ge(consts_ready, 2 + NS)
            for q in range(PAIRS):
                first_scores(0, 0, q, 1)
            for q in range(EARLY):
                first_scores(1, 1, q, 1)
            for t in range(HEAD):
                slot(0, 0, t, load=1)
            with pe.Fori(0, PE_LOOPS) as i:
                for s in range(BODY):
                    group(i, s, 2)
            for n in range(PE_LOOPS * BODY, NG):
                group(n // BODY, n % BODY, NG - 1 - n)


def output(nc, a_scr, wo, ao, bo, x, out):
    QT, NN = Q // P, H // BANK
    UN = QT * NN
    with ExitStack() as ctx:
        sb = lambda n, s, d: ctx.enter_context(nc.sbuf_tensor(n, s, d))
        sem = lambda n: ctx.enter_context(nc.semaphore(n))
        w_done = sem("wo_done")
        w, w_units, w_load, w_products, w_high, w_low = fold_weights(nc, ctx, "wo", H, [(ao, bo, wo, 0)], w_done)
        parts = [sb(f"a_parts{i}", [P, NKV, 2 * Q], F32R) for i in range(2)]
        res = sb("res", [P, QT, H], F32)
        banks = [ctx.enter_context(nc.psum_tensor(f"o_bank{i}", [P, BANK], F32)) for i in range(UN)]
        a_loaded = [sem(f"a_loaded{i}") for i in range(2)]
        x_loaded, o_ready, o_added, o_stored = sem("res_loaded"), sem("o_ready"), sem("o_added"), sem("o_stored")
        block = ctx.enter_context(nc.Block())

        @block.sync
        def _(sp):
            w_load(sp)
            with sp.Fori(0, B // 2) as bb:
                for half in range(2):
                    b = bb * 2 + half
                    sp.wait_ge(o_ready, (b + 1) * UN)
                    sp.dma_start(parts[half][:, :, :].bitcast(F32), a_scr[bass.ds(b * NKV, NKV), :, :, :].rearrange(
                        "g p c q -> p g (c q)")).then_inc(a_loaded[half], 16)

        @block.scalar
        def _(act):
            act.sem_inc(o_stored, 16)
            w_high(act)
            with act.Fori(0, B) as b:
                act.wait_ge(o_stored, (b + 1) * 16)
                act.dma_start(res[:, :, :], x[bass.ds(b, 1), :, :].rearrange(
                    "o (t p) n -> (o p) t n", p=P)).then_inc(x_loaded, 16)
                act.wait_ge(o_added, (b + 2) * UN)
                act.dma_start(out[bass.ds(b, 1), :, :].rearrange("o (t p) n -> (o p) t n", p=P),
                              res[:, :, :]).then_inc(o_stored, 16)
            act.wait_ge(o_stored, (B + 1) * 16)

        @block.vector
        def _(dve):
            dve.sem_inc(o_added, UN)
            w_low(dve, banks)
            with dve.Fori(0, B) as b:
                dve.wait_ge(x_loaded, (b + 1) * 16)
                for u in range(UN):
                    qt, nn = divmod(u, NN)
                    dve.wait_ge(o_ready, (b + 2) * UN + u + 1)
                    r = res[:, qt, nn * BANK:(nn + 1) * BANK]
                    nc.vector.tensor_tensor(r, banks[u][:, :], r, ALU.add).then_inc(o_added, 1)

        @block.tensor
        def _(pe):
            pe.sem_inc(o_ready, 2 * UN)
            w_products(pe, banks)
            pe.wait_ge(w_done, w_units)
            with pe.Fori(0, B // 2) as bb:
                for half in range(2):
                    b = bb * 2 + half
                    pe.wait_ge(a_loaded[half], (bb + 1) * 16)
                    for u in range(UN):
                        qt, nn = divmod(u, NN)
                        pe.wait_ge(o_added, b * UN + u + 1)
                        for i, (k, (xp, wp)) in enumerate((k, t) for k in range(KT) for t in TERMS):
                            q0 = xp * Q + qt * P
                            last = nc.tensor.matmul(banks[u][:, :], parts[half][:, k, q0:q0 + P],
                                                    w[:, k, wp, nn * BANK:(nn + 1) * BANK], start=i == 0,
                                                    stop=i == KT * len(TERMS) - 1)
                        last.then_inc(o_ready, 1)


def build(nc, xT, x, ctxT, wq, aq, bq, wk, ak, bk, wv, av, bv, wo, ao, bo, out):
    k_scr = nc.dram_tensor("k_scr", (B * KV, 2, TP), F32).ap()
    v_scr = nc.dram_tensor("v_scr", (NG, P, NT * HD), F32).ap()
    q_scr = nc.dram_tensor("q_scr", (B * H, 2, Q), F32).ap()
    a_scr = nc.dram_tensor("a_scr", (NG, P, 2, Q), F32).ap()
    keys_and_values(nc, ctxT, wk, ak, bk, wv, av, bv, k_scr, v_scr)
    queries(nc, xT, wq, aq, bq, q_scr)
    attention(nc, k_scr, v_scr, q_scr, a_scr)
    output(nc, a_scr, wo, ao, bo, x, out)


def kernel(**inputs):
    import concourse.bacc as bacc
    from concourse.bass_utils import run_bass_kernel_spmd

    g = {k.replace("L0_xattn_", ""): np.asarray(v) for k, v in inputs.items()}
    ctx = g["ctx_4096"]
    arrays = {
        "xT": g["x"].transpose(0, 2, 1),
        "x": g["x"],
        "ctxT": np.pad(ctx, ((0, 0), (0, TP - T), (0, 0)), mode="edge").transpose(0, 2, 1),
    }
    for s in "qkvo":
        arrays[f"W{s}"], arrays[f"A{s}T"], arrays[f"B{s}"] = g[f"W{s}"], g[f"A{s}"].T, g[f"B{s}"]
    arrays = {f"in_{k}": np.ascontiguousarray(v) for k, v in arrays.items()}
    nc = bacc.Bacc("TRN2", target_bir_lowering=False, num_devices=1)
    args = [nc.dram_tensor(k, v.shape, mybir.dt.from_np(v.dtype), kind="ExternalInput").ap() for k, v in arrays.items()]
    out = nc.dram_tensor("out", (B, Q, H), F32, kind="ExternalOutput").ap()
    build(nc, *args, out)
    return run_bass_kernel_spmd(nc, [arrays], core_ids=[0]).results[0]["out"]
```

```python
from contextlib import ExitStack

import numpy as np
import concourse.bass as bass
from concourse import mybir

F32 = mybir.dt.float32
F32R = mybir.dt.float32r
ALU = mybir.AluOpType
ACT = mybir.ActivationFunctionType
AX = mybir.AxisListType

B, Q, T, H = 4, 512, 1601, 1024
NH, NKV, R = 32, 8, 16
HD = H // NH
KV = NKV * HD
GH = NH // NKV
NG = B * NKV
LORA_SCALE = 2.0
P = 128
KT = H // P
NT = -(-T // P)
TP = NT * P
TL = T - (NT - 1) * P
BANK = 512
SCALE = float(HD) ** -0.5
TERMS = ((0, 0), (0, 1), (1, 0))


class FoldedWeights:

    def __init__(self, nc, ctx, name, cols, pairs, banks):
        sb = lambda n, s, d: ctx.enter_context(nc.sbuf_tensor(f"{name}_{n}", s, d))
        sem = lambda n: ctx.enter_context(nc.semaphore(f"{name}_{n}"))
        self.nc, self.pairs, self.banks = nc, pairs, banks
        self.at, self.lb = sb("at", [R, len(pairs), H], F32), sb("lb", [R, cols], F32)
        self.raw, self.parts = sb("raw", [P, KT, cols], F32), sb("parts", [P, KT, 2, cols], F32R)
        self.units = [(k, c) for c in range(0, cols, BANK) for k in range(KT)]
        self.lora_loaded = sem("lora_loaded")
        self.tile_loaded = [sem(f"tile_loaded{u}") for u in range(len(self.units))]
        self.ab_ready, self.summed, self.hi_done, self.done = sem("ab_ready"), sem("summed"), sem("hi_done"), sem("done")

    def pieces(self, c):
        for j, (_, b, _, c0) in enumerate(self.pairs):
            lo, hi = max(c, c0), min(c + BANK, c0 + b.shape[1])
            if lo < hi:
                yield j, c0, lo, hi

    def load_lora(self, sp):
        for j, (a, b, _, c0) in enumerate(self.pairs):
            sp.dma_start(self.at[:, j, :], a).then_inc(self.lora_loaded, 16)
            sp.dma_start(self.lb[:, c0:c0 + b.shape[1]], b).then_inc(self.lora_loaded, 16)

    def load(self, sp, u):
        k, c = self.units[u]
        for j, c0, lo, hi in self.pieces(c):
            sp.dma_start(self.raw[:, k, lo:hi],
                         self.pairs[j][2][k * P:(k + 1) * P, lo - c0:hi - c0]).then_inc(self.tile_loaded[u], 16)

    def product(self, pe, u):
        k, c = self.units[u]
        if u == 0:
            pe.wait_ge(self.lora_loaded, 32 * len(self.pairs))
        if u >= len(self.banks):
            pe.wait_ge(self.summed, u - len(self.banks) + 1)
        for j, _, lo, hi in self.pieces(c):
            last = self.nc.tensor.matmul(self.banks[u % len(self.banks)][:, lo - c:hi - c],
                                         self.at[:, j, k * P:(k + 1) * P], self.lb[:, lo:hi], start=True, stop=True)
        last.then_inc(self.ab_ready, 1)

    def add(self, dve, u):
        k, c = self.units[u]
        dve.wait_ge(self.tile_loaded[u], 16 * len(list(self.pieces(c))))
        dve.wait_ge(self.ab_ready, u + 1)
        self.nc.vector.scalar_tensor_tensor(out=self.raw[:, k, c:c + BANK], in0=self.banks[u % len(self.banks)][:, :],
                                            scalar=LORA_SCALE, in1=self.raw[:, k, c:c + BANK],
                                            op0=ALU.mult, op1=ALU.add).then_inc(self.summed, 1)

    def high(self, act, u):
        k, c = self.units[u]
        act.wait_ge(self.summed, u + 1)
        self.nc.scalar.activation(self.parts[:, k, 0, c:c + BANK], self.raw[:, k, c:c + BANK],
                                  ACT.Copy).then_inc(self.hi_done, 1)

    def low(self, dve, u):
        k, c = self.units[u]
        dve.wait_ge(self.hi_done, u + 1)
        self.nc.vector.tensor_tensor(self.parts[:, k, 1, c:c + BANK], self.raw[:, k, c:c + BANK],
                                     self.parts[:, k, 0, c:c + BANK].bitcast(F32), ALU.subtract).then_inc(self.done, 1)


def keys_and_values(nc, ctxT, wk, ak, bk, wv, av, bv, k_scr, v_scr):
    NC = -(-TP // BANK)
    assert NC % 2 == 0
    ends = [-(-NT * (c + 1) // NC) for c in range(NC)]
    starts = [0] + ends[:-1]
    widths = [(e - a) * P for a, e in zip(starts, ends)]
    MK = KV // P
    with ExitStack() as ctx:
        sb = lambda n, s, d: ctx.enter_context(nc.sbuf_tensor(n, s, d))
        sem = lambda n: ctx.enter_context(nc.semaphore(n))
        raw = [sb(f"ctx_raw{i}", [P, KT, BANK], F32) for i in range(2)]
        parts = [sb(f"ctx_parts{i}", [P, 2, KT, BANK], F32R) for i in range(2)]
        k_out = [sb(f"k_out{i}", [P, 2, BANK], F32R) for i in range(MK)]
        v_out = sb("v_out", [P, NKV, NT, HD], F32)
        banks = [ctx.enter_context(nc.psum_tensor(f"kv_bank{i}", [P, BANK], F32)) for i in range(8)]
        k_bank, v_bank = banks[0:4], banks[4:8]
        fold = FoldedWeights(nc, ctx, "wkv", 2 * KV, [(ak, bk, wk, 0), (av, bv, wv, KV)], k_bank[MK:])
        w = fold.parts
        assert len(fold.units) == KT and ends[0] == len(v_bank)
        ctx_loaded = [sem(f"ctx_loaded{k}") for k in range(KT)]
        ctx_hi, ctx_lo = sem("ctx_hi"), sem("ctx_lo")
        k_ready, k_hi, k_lo = sem("k_ready"), sem("k_hi"), sem("k_lo")
        v_ready, v_hi, v_copied = sem("v_ready"), sem("v_hi"), sem("v_copied")
        k_stored, v_stored = [sem(f"k_stored{i}") for i in range(MK)], sem("v_stored")
        block = ctx.enter_context(nc.Block())

        def by_head(columns):
            return columns.rearrange("p (g d) -> p g d", g=NKV)

        def v_tiles_before(b, c):
            return b * NT + (ends[c - 2] + NT if c >= 2 else ends[c - 2])

        @block.sync
        def _(sp):
            def load(b, c, fold=None):
                for k in range(KT):
                    if fold:
                        fold.load(sp, k)
                    sp.wait_ge(ctx_lo, (b * NC + c - 1 + NC) * KT + k + 1)
                    sp.dma_start(raw[c % 2][:, k, 0:widths[c]],
                                 ctxT[bass.ds(b, 1), k * P:(k + 1) * P, starts[c] * P:ends[c] * P].rearrange(
                                     "o p t -> (o p) t")).then_inc(ctx_loaded[k], 16)

            def store_values(b, t0, t1):
                sp.wait_ge(v_copied, b * NT + t1 + NT)
                sp.dma_start(v_scr[bass.ds(b * NKV, NKV), :, t0 * HD:t1 * HD].rearrange("g p f -> p g f"),
                             v_out[:, :, t0:t1, :].rearrange("p g t d -> p g (t d)")).then_inc(v_stored, 16)

            def batch(b, last):
                for c in range(NC):
                    if c + 1 < NC:
                        load(b, c + 1)
                    elif not last:
                        load(b + 1, 0)
                    for m in range(MK):
                        sp.wait_ge(k_lo, b * (NC * MK) + c * MK + m + 1 + 4)
                        sp.dma_start(k_scr[bass.ds(b * KV + m * P, P), :, starts[c] * P:ends[c] * P],
                                     k_out[m][:, :, 0:widths[c]].bitcast(F32)).then_inc(k_stored[m], 16)
                    if c == NC - 2:
                        store_values(b, 0, ends[c])
                store_values(b, starts[NC - 1], NT)

            fold.load_lora(sp)
            load(0, 0, fold)
            with sp.Fori(0, B - 1) as b:
                batch(b, False)
            batch(B - 1, True)
            for m in range(MK):
                sp.wait_ge(k_stored[m], (B * NC + 1) * 16)
            sp.wait_ge(v_stored, (B + 1) * 32)

        @block.scalar
        def _(act):
            def split(b, c, fold=None):
                n = widths[c]
                act.wait_ge(v_ready, v_tiles_before(b, c))
                for k in range(KT):
                    act.wait_ge(ctx_loaded[k], (b * NC + c + 1) * 16)
                    nc.scalar.activation(parts[c % 2][:, 0, k, 0:n], raw[c % 2][:, k, 0:n], ACT.Copy).then_inc(ctx_hi, 1)
                    if fold:
                        fold.high(act, k)

            def batch(b, last):
                for c in range(NC):
                    n = widths[c]
                    for m in range(MK):
                        u = b * (NC * MK) + c * MK + m
                        act.wait_ge(k_ready, u + 1)
                        act.wait_ge(k_stored[m], (b * NC + c + 1) * 16)
                        nc.scalar.activation(k_out[m][:, 0, 0:n], k_bank[(c * MK + m) % 4][:, 0:n],
                                             ACT.Copy).then_inc(k_hi, 1)
                    if c + 1 < NC:
                        split(b, c + 1)
                    elif not last:
                        split(b + 1, 0)
                    for t in range(starts[c], ends[c]):
                        act.wait_ge(v_ready, b * NT + t + 1 + NT)
                        if t == 0:
                            act.wait_ge(v_stored, (b + 1) * 32)
                        nc.scalar.activation(v_out[:, :, t, :], by_head(v_bank[t % 4][:, 0:KV]),
                                             ACT.Copy).then_inc(v_hi, 1)

            act.sem_inc(v_stored, 32)
            for m in range(MK):
                act.sem_inc(k_stored[m], 16)
            split(0, 0, fold)
            with act.Fori(0, B - 1) as b:
                batch(b, False)
            batch(B - 1, True)

        @block.vector
        def _(dve):
            def split(b, c, fold=None):
                n = widths[c]
                for k in range(KT):
                    if fold:
                        fold.add(dve, k)
                    dve.wait_ge(ctx_hi, (b * NC + c) * KT + k + 1)
                    nc.vector.tensor_tensor(parts[c % 2][:, 1, k, 0:n], raw[c % 2][:, k, 0:n],
                                            parts[c % 2][:, 0, k, 0:n].bitcast(F32), ALU.subtract).then_inc(ctx_lo, 1)
                    if fold:
                        fold.low(dve, k)

            def batch(b, last):
                for c in range(NC):
                    n = widths[c]
                    for m in range(MK):
                        u = b * (NC * MK) + c * MK + m
                        dve.wait_ge(k_hi, u + 1)
                        nc.vector.tensor_tensor(k_out[m][:, 1, 0:n], k_bank[(c * MK + m) % 4][:, 0:n],
                                                k_out[m][:, 0, 0:n].bitcast(F32), ALU.subtract).then_inc(k_lo, 1)
                    if c + 1 < NC:
                        split(b, c + 1)
                    elif not last:
                        split(b + 1, 0)
                    for t in range(starts[c], ends[c]):
                        dve.wait_ge(v_hi, b * NT + t + 1)
                        nc.vector.tensor_tensor(v_out[:, :, t, :], by_head(v_bank[t % 4][:, KV:2 * KV]),
                                                v_out[:, :, t, :], ALU.add).then_inc(v_copied, 1)

            dve.sem_inc(v_copied, NT)
            dve.sem_inc(ctx_lo, NC * KT)
            dve.sem_inc(k_lo, 4)
            split(0, 0, fold)
            with dve.Fori(0, B - 1) as b:
                batch(b, False)
            batch(B - 1, True)

        @block.tensor
        def _(pe):
            def k_product(c, m, k):
                n, x = widths[c], parts[c % 2]
                for i, (wp, xp) in enumerate(TERMS):
                    last = nc.tensor.matmul(k_bank[(c * MK + m) % 4][:, 0:n], w[:, k, wp, m * P:(m + 1) * P],
                                            x[:, xp, k, 0:n], start=k == 0 and i == 0,
                                            stop=k == KT - 1 and i == len(TERMS) - 1)
                if k == KT - 1:
                    last.then_inc(k_ready, 1)

            def v_product(c, t, k):
                x, t0 = parts[c % 2], (t - starts[c]) * P
                nc.tensor.matmul(v_bank[t % 4][:, :], x[:, 0, k, t0:t0 + P], w[:, k, :, KV:2 * KV],
                                 start=k == 0, stop=k == KT - 1)
                last = nc.tensor.matmul(v_bank[t % 4][:, 0:KV], x[:, 1, k, t0:t0 + P], w[:, k, 0, KV:2 * KV],
                                        start=False, stop=k == KT - 1, skip_group_check=True)
                if k == KT - 1:
                    last.then_inc(v_ready, 1)

            def chunk(b, c):
                for m in range(MK):
                    pe.wait_ge(k_lo, b * (NC * MK) + c * MK + m + 1)
                    for k in range(KT):
                        if m == 0:
                            pe.wait_ge(ctx_lo, (b * NC + c + NC) * KT + k + 1)
                        k_product(c, m, k)
                for t in range(starts[c], ends[c]):
                    used = t - 4 + NT if t >= 4 else (NT - 1 - (NT - 1 - t) % 4)
                    pe.wait_ge(v_copied, b * NT + used + 1)
                    for k in range(KT):
                        v_product(c, t, k)

            pe.sem_inc(v_ready, NT)
            for k in range(len(fold.banks)):
                fold.product(pe, k)
            for k in range(KT):
                pe.wait_ge(fold.done, k + 1)
                pe.wait_ge(ctx_lo, NC * KT + k + 1)
                for m in range(MK):
                    k_product(0, m, k)
                for t in range(ends[0]):
                    v_product(0, t, k)
                if k + len(fold.banks) < KT:
                    fold.product(pe, k + len(fold.banks))
            for c in range(1, NC):
                chunk(0, c)
            with pe.Fori(1, B) as b:
                for c in range(NC):
                    chunk(b, c)


def queries(nc, xT, wq, aq, bq, q_scr):
    MQ = H // P
    with ExitStack() as ctx:
        sb = lambda n, s, d: ctx.enter_context(nc.sbuf_tensor(n, s, d))
        sem = lambda n: ctx.enter_context(nc.semaphore(n))
        raw = sb("x_raw", [P, KT, Q], F32)
        parts = [sb(f"x_parts{i}", [P, 2, KT, Q], F32R) for i in range(2)]
        q_out = [sb(f"q_out{i}", [P, 2, Q], F32R) for i in range(2)]
        banks = [ctx.enter_context(nc.psum_tensor(f"q_bank{i}", [P, Q], F32)) for i in range(MQ)]
        HALF = MQ // 2
        fold = FoldedWeights(nc, ctx, "wq", H, [(aq, bq, wq, 0)], banks[HALF:])
        w, UNITS = fold.parts, len(fold.units)
        assert UNITS == 2 * KT and HALF * P == BANK
        x_loaded = [sem(f"x_loaded{k}") for k in range(KT)]
        x_hi, x_lo = sem("x_hi"), sem("x_lo")
        q_ready, q_hi, q_lo = sem("q_ready"), sem("q_hi"), sem("q_lo")
        q_stored = [sem(f"q_stored{i}") for i in range(2)]
        block = ctx.enter_context(nc.Block())

        def evacuations(bb, half):
            return [((bb * 2 + half) * MQ + m, m, m % 2, (bb * 2 + half) * (MQ // 2) + m // 2) for m in range(MQ)]

        @block.sync
        def _(sp):
            def load(b, fold=None):
                for k in range(KT):
                    if fold:
                        fold.load(sp, k)
                    if not (isinstance(b, int) and b == 0):
                        sp.wait_ge(x_lo, (b - 1) * KT + k + 1)
                    sp.dma_start(raw[:, k, :], xT[bass.ds(b, 1), k * P:(k + 1) * P, :].rearrange(
                        "o p t -> (o p) t")).then_inc(x_loaded[k], 16)

            def batch(b, more):
                if more:
                    load(b + 2)
                for m in range(MQ):
                    sp.wait_ge(q_lo, b * MQ + m + 1 + MQ)
                    sp.dma_start(q_scr[bass.ds(b * H + m * P, P), :, :],
                                 q_out[m % 2][:, :, :].bitcast(F32)).then_inc(q_stored[m % 2], 16)

            fold.load_lora(sp)
            load(0, fold)
            for u in range(KT, UNITS):
                fold.load(sp, u)
            load(1)
            with sp.Fori(0, B - 2) as b:
                batch(b, True)
            batch(B - 2, False)
            batch(B - 1, False)
            for s in range(2):
                sp.wait_ge(q_stored[s], (B * (MQ // 2) + 1) * 16)

        @block.scalar
        def _(act):
            for s in range(2):
                act.sem_inc(q_stored[s], 16)

            def split(bb, half, fold=None):
                act.wait_ge(q_ready, (bb * 2 + half + 1) * MQ)
                for k in range(KT):
                    act.wait_ge(x_loaded[k], (bb * 2 + half + 1) * 16)
                    nc.scalar.activation(parts[half][:, 0, k], raw[:, k, :], ACT.Copy).then_inc(x_hi, 1)
                    if fold:
                        fold.high(act, k)

            def batch(bb, half):
                for u, m, s, stores in evacuations(bb, half):
                    act.wait_ge(q_ready, u + 1 + 2 * MQ)
                    act.wait_ge(q_stored[s], (stores + 1) * 16)
                    nc.scalar.activation(q_out[s][:, 0, :], banks[m][:, :], ACT.Copy).then_inc(q_hi, 1)

            split(0, 0, fold)
            for u in range(KT, UNITS):
                fold.high(act, u)
            with act.Fori(0, B // 2 - 1) as bb:
                split(bb, 1)
                batch(bb, 0)
                split(bb + 1, 0)
                batch(bb, 1)
            split(B // 2 - 1, 1)
            batch(B // 2 - 1, 0)
            batch(B // 2 - 1, 1)

        @block.vector
        def _(dve):
            dve.sem_inc(q_lo, MQ)

            def split(bb, half, fold=None):
                for k in range(KT):
                    if fold:
                        fold.add(dve, k)
                    dve.wait_ge(x_hi, (bb * 2 + half) * KT + k + 1)
                    nc.vector.tensor_tensor(parts[half][:, 1, k], raw[:, k, :], parts[half][:, 0, k].bitcast(F32),
                                            ALU.subtract).then_inc(x_lo, 1)
                    if fold:
                        fold.low(dve, k)

            def batch(bb, half):
                for u, m, s, _ in evacuations(bb, half):
                    dve.wait_ge(q_hi, u + 1)
                    nc.vector.tensor_tensor(q_out[s][:, 1, :], banks[m][:, :], q_out[s][:, 0, :].bitcast(F32),
                                            ALU.subtract).then_inc(q_lo, 1)

            split(0, 0, fold)
            for u in range(KT, UNITS):
                fold.add(dve, u)
                if u > KT:
                    fold.low(dve, u - 1)
            fold.low(dve, UNITS - 1)
            with dve.Fori(0, B // 2 - 1) as bb:
                split(bb, 1)
                batch(bb, 0)
                split(bb + 1, 0)
                batch(bb, 1)
            split(B // 2 - 1, 1)
            batch(B // 2 - 1, 0)
            batch(B // 2 - 1, 1)

        @block.tensor
        def _(pe):
            def product(half, m, k):
                for i, (wp, xp) in enumerate(TERMS):
                    last = nc.tensor.matmul(banks[m][:, :], w[:, k, wp, m * P:(m + 1) * P], parts[half][:, xp, k, :],
                                            start=k == 0 and i == 0, stop=k == KT - 1 and i == len(TERMS) - 1)
                if k == KT - 1:
                    last.then_inc(q_ready, 1)

            def batch(bb, half):
                for u, m, _, _ in evacuations(bb, half):
                    pe.wait_ge(q_lo, u + 1)
                    for k in range(KT):
                        if m == 0:
                            pe.wait_ge(x_lo, (bb * 2 + half) * KT + k + 1)
                        product(half, m, k)

            pe.sem_inc(q_ready, 2 * MQ)
            for u in range(len(fold.banks)):
                fold.product(pe, u)
            for u, (k, c) in enumerate(fold.units):
                pe.wait_ge(fold.done, u + 1)
                if c == 0:
                    pe.wait_ge(x_lo, k + 1)
                for m in range(c // P, c // P + HALF):
                    if c and k == 0:
                        pe.wait_ge(fold.summed, UNITS - MQ + m + 1)
                    product(0, m, k)
                if c == 0:
                    fold.product(pe, u + len(fold.banks))
                if u == KT - 1:
                    for rest in range(KT + len(fold.banks), UNITS):
                        fold.product(pe, rest)
            batch(0, 1)
            with pe.Fori(1, B // 2) as bb:
                for half in range(2):
                    batch(bb, half)


def attention(nc, k_scr, v_scr, q_scr, a_scr):
    S3 = 3 * HD
    QT = Q // P
    UNITS = GH * QT
    CH = 402
    NCH = 4
    assert CH % 2 == 0 and T <= NCH * CH <= TP
    PAIRS = UNITS * NCH // 2
    NS = 3
    HEAD = 5
    ORDER = ["DPCP01P23P", "0P1CP23PD", "0P1CP23P", "0P1CP23PD", "0P1CP23PD"] + ["0P1C23P"] * 6 + ["0N1C23N"] * 2
    EARLY = sum(o.count("N") for o in ORDER)
    BEFORE = [EARLY + sum(o.count("P") for o in ORDER[:t]) for t in range(NT + 1)]
    assert len(ORDER) == NT and BEFORE[NT] == PAIRS
    assert not any("N" in o and "P" in "".join(ORDER[t:]) for t, o in enumerate(ORDER))
    EARLY_BEFORE = [sum(o.count("N") for o in ORDER[:t]) for t in range(NT + 1)]
    TURN = max(t for t, o in enumerate(ORDER) if "P" in o)
    RECIP_SLOTS = (5, 5, 6, 7, 8, 9, 10, 12)
    RECIPS = len(RECIP_SLOTS)
    BANK_OF = [j % 2 if j < HEAD * GH else (j - HEAD * GH) % 3 for j in range(GH * NT)]
    RUNS = ((0, 1, 2, 3), (4, 5, 6, 7), (8, 9, 10))
    ADDS = sum(len(r) - 1 for r in RUNS)
    ADDED_AT = {t: sum(len(x) - 1 for x in RUNS[:j]) + max(i, 1) for j, r in enumerate(RUNS) for i, t in enumerate(r)}
    TAIL_SLOTS = (1, 2, 3, 3)
    BLOCKS = ((0, NT), (1, NT + 1), (2, NT + 3), (None, NT + 4))
    LAST_RUN = len(RUNS) - 1
    BLOCK_OF = {x: i + 1 for i, (x, _) in enumerate(BLOCKS)}
    TILES = GH * NT
    SB = len(BLOCKS)
    BODY = 3
    assert all("D" in ORDER[at % NT] for _, at in BLOCKS)
    assert all(t in ADDED_AT for t in range(NT - 2))
    PE_LOOPS = (NG - 2) // BODY
    SP_LOOPS = (NG - NS) // BODY

    with ExitStack() as ctx:
        sb = lambda n, s, d: ctx.enter_context(nc.sbuf_tensor(n, s, d))
        ps = lambda n, s: ctx.enter_context(nc.psum_tensor(n, s, F32))
        sem = lambda n: ctx.enter_context(nc.semaphore(n))
        k_stack = [sb(f"k_stack{i}", [S3 + 1, TP], F32R) for i in range(NS)]
        q_stack = [sb(f"q_stack{i}", [S3 + 1, GH * Q], F32R) for i in range(NS)]
        values = [sb(f"values{i}", [P, NT * HD], F32) for i in range(NS)]
        ones = sb("ones", [P, HD], F32)
        probs = [sb(f"probs{t}", [P, GH * Q], F32) for t in range(NT)]
        run_sum = [sb(f"run_sum{i}", [P, GH * Q], F32) for i in range(len(RUNS))]
        part_max = sb("part_max", [P, UNITS, 2], F32)
        neg_max = sb("neg_max", [P, HD], F32R)
        neg_max_t = sb("neg_max_t", [P, HD], F32)
        context, denom = sb("context", [P, Q], F32), sb("denom", [P, Q], F32)
        recip, attn = sb("recip", [P, Q], F32), sb("attn", [P, Q], F32)
        attn_parts = sb("attn_parts", [P, 2, Q], F32R)
        first = ps("first", [P, NCH, BANK])
        second = [ps(f"second{i}", [P, BANK]) for i in range(3)]
        context_ps, denom_ps = ps("context_ps", [P, Q]), second[2]

        consts_ready = sem("consts_ready")
        stacked = [sem(f"stacked{i}") for i in range(NS)]
        first_ready, first_read = sem("first_ready"), sem("first_read")
        neg_ready, neg_turned, neg_stacked = sem("neg_ready"), sem("neg_turned"), sem("neg_stacked")
        second_ready, exp_done = sem("second_ready"), sem("exp_done")
        context_done, denom_done = sem("context_done"), sem("denom_done")
        added, tail_added = sem("added"), sem("tail_added")
        context_copied, denom_copied = sem("context_copied"), sem("denom_copied")
        recip_done, attn_done, hi_done, lo_done = sem("recip_done"), sem("attn_done"), sem("a_hi_done"), sem("a_lo_done")
        attn_stored = sem("attn_stored")
        block = ctx.enter_context(nc.Block())

        LOADS = 7

        def exps(n, t):
            return n * TILES + (t + 1) * GH + 2

        @block.sync
        def _(sp):
            def load(n, s):
                kr = k_scr[bass.ds(n * HD, HD), :, :]
                qr = q_scr[bass.ds(n * P, P), :, :].rearrange("(h d) c q -> d c h q", d=HD)
                for r, part in enumerate((0, 0, 1)):
                    sp.dma_start(k_stack[s][r * HD:(r + 1) * HD, :].bitcast(F32), kr[:, part, :]).then_inc(stacked[s], 16)
                for r, part in enumerate((0, 1, 0)):
                    sp.dma_start(q_stack[s][r * HD:(r + 1) * HD, :].bitcast(F32).rearrange("d (h q) -> d h q", h=GH),
                                 qr[:, part]).then_inc(stacked[s], 16)

            def load_values(n, s):
                sp.dma_start(values[s][:, :], v_scr[bass.ds(n, 1), :, :].rearrange("o p f -> (o p) f")).then_inc(stacked[s], 16)

            def stack_max(n, s):
                sp.wait_ge(neg_turned, n + 1)
                row = q_stack[s][S3:S3 + 1, :].bitcast(F32).rearrange("o (u i c) -> o i u c", i=P // HD, c=HD)
                for i in range(P // HD):
                    sp.dma_start(row[:, i], neg_max_t[i * HD:i * HD + UNITS, :]).then_inc(neg_stacked, 16)

            def store(n):
                sp.wait_ge(lo_done, n + 2)
                sp.dma_start(a_scr[bass.ds(n, 1), :, :, :].rearrange("o p c q -> (o p) c q"),
                             attn_parts[:, :, :].bitcast(F32)).then_inc(attn_stored, 16)

            def group(n, s):
                known = isinstance(n, int)
                if not (known and n + 1 >= NG):
                    stack_max(n + 1, (s + 1) % NS)
                if not (known and n + NS >= NG):
                    sp.wait_ge(second_ready, (n + 1) * TILES)
                    load(n + NS, s)
                    sp.wait_ge(context_done, (n + 2) * NT)
                    load_values(n + NS, s)
                if not (known and n == 0):
                    store(n - 1)

            for n in range(NS):
                load(n, n)
                load_values(n, n)
            stack_max(0, 0)
            for n in range(BODY):
                group(n, n)
            with sp.Fori(1, SP_LOOPS) as i:
                for s in range(BODY):
                    group(i * BODY + s, s)
            for n in range(SP_LOOPS * BODY, NG):
                group(n, n % NS)
            store(NG - 1)
            sp.wait_ge(attn_stored, (NG + 1) * 16)

        @block.gpsimd
        def _(pool):
            def add_runs(n, runs=RUNS):
                count = 0
                for j, run in enumerate(runs):
                    pool.wait_ge(denom_done, n * SB + BLOCK_OF[j])
                    for i in range(1, len(run)):
                        pool.wait_ge(exp_done, exps(n, run[i]))
                        if i > 1:
                            pool.wait_ge(added, (n + 1) * ADDS + count)
                        nc.gpsimd.tensor_tensor(run_sum[j][:, :], (probs[run[0]] if i == 1 else run_sum[j])[:, :],
                                                probs[run[i]][:, :], ALU.add).then_inc(added, 1)
                        count += 1

            def low_part(n):
                pool.wait_ge(hi_done, n + 1)
                nc.gpsimd.tensor_tensor(attn_parts[:, 1, :], attn[:, :], attn_parts[:, 0, :].bitcast(F32),
                                        ALU.subtract).then_inc(lo_done, 1)

            pool.sem_inc(added, ADDS)
            add_runs(0)
            with pool.Fori(1, NG - 1) as n:
                add_runs(n)
                low_part(n - 1)
            add_runs(NG - 1, RUNS[:LAST_RUN])
            low_part(NG - 2)
            low_part(NG - 1)

        @block.scalar
        def _(act):
            act.sem_inc(exp_done, 2)

            def tile(n, t):
                rows = P if t < NT - 1 else TL
                act.wait_ge(context_done, n * NT + t + 1)
                if t in ADDED_AT:
                    act.wait_ge(added, n * ADDS + ADDED_AT[t])
                else:
                    act.wait_ge(denom_done, n * SB + BLOCK_OF[None])
                for h in range(GH):
                    act.wait_ge(second_ready, n * TILES + t * GH + h + 1)
                    nc.scalar.activation(probs[t][0:rows, h * Q:(h + 1) * Q], second[BANK_OF[t * GH + h]][0:rows, :],
                                         ACT.Exp, scale=SCALE).then_inc(exp_done, 1)

            def copy_context(n):
                act.wait_ge(context_done, (n + 2) * NT)
                act.wait_ge(attn_done, n + 1)
                nc.scalar.activation(context[:, :], context_ps[:, :], ACT.Copy).then_inc(context_copied, 1)

            def copy_denom(n):
                act.wait_ge(denom_done, (n + 2) * SB)
                nc.scalar.activation(denom[:, :], denom_ps[:, :], ACT.Copy).then_inc(denom_copied, 1)

            def high_part(n):
                act.wait_ge(attn_done, n + 2)
                act.wait_ge(attn_stored, (n + 1) * 16)
                nc.scalar.activation(attn_parts[:, 0, :], attn[:, :], ACT.Copy).then_inc(hi_done, 1)

            for t in range(HEAD):
                tile(0, t)

            def group(n, divided=True):
                for t in range(HEAD, NT):
                    tile(n, t)
                copy_context(n)
                for t in range(HEAD):
                    tile(n + 1, t)
                    if t == 0 and divided:
                        high_part(n - 1)
                copy_denom(n)

            group(0, divided=False)
            with act.Fori(1, NG - 1) as n:
                group(n)
            for t in range(HEAD, NT):
                tile(NG - 1, t)
            copy_context(NG - 1)
            high_part(NG - 2)
            copy_denom(NG - 1)
            high_part(NG - 1)

        @block.vector
        def _(dve):
            dve.sem_inc(attn_done, 1)
            dve.sem_inc(lo_done, 1)
            dve.sem_inc(attn_stored, 16)
            nc.vector.memset(ones[:, :], 1.0).then_inc(consts_ready, 1)
            nc.vector.memset(neg_max[:, :].bitcast(F32), 0.0).then_inc(consts_ready, 1)
            for s in range(NS):
                nc.vector.memset(k_stack[s][S3:S3 + 1, :].bitcast(F32), 1.0).then_inc(consts_ready, 1)

            def read_pairs(n, pairs):
                for q in pairs:
                    dve.wait_ge(first_ready, n * PAIRS + q + 1)
                    half = q % 2
                    nc.vector.tensor_reduce(part_max[:, q // 2, half:half + 1], first[:, 2 * half:2 * half + 2, 0:CH],
                                            AX.XY, ALU.max).then_inc(first_read, 1)

            def add_tail(n, h):
                if h == 0:
                    dve.wait_ge(exp_done, exps(n, NT - 1))
                    dve.wait_ge(context_done, (n + 2) * NT - 1)
                cols = slice(h * Q, (h + 1) * Q)
                nc.vector.tensor_tensor(probs[NT - 2][0:TL, cols], probs[NT - 2][0:TL, cols], probs[NT - 1][0:TL, cols],
                                        ALU.add).then_inc(tail_added, 1)

            def finish_max(n):
                dve.wait_ge(first_read, (n + 1) * PAIRS)
                nc.vector.tensor_reduce(neg_max[:, 0:UNITS], part_max[:, :, :], AX.X, ALU.max,
                                        negate=True).then_inc(neg_ready, 1)
                dve.wait_ge(neg_ready, n + 1)
                if not (isinstance(n, int) and n == 0):
                    dve.wait_ge(neg_stacked, n * (P // HD) * 16)
                nc.vector.transpose(neg_max_t[:, :], neg_max[:, :].bitcast(F32)).then_inc(neg_turned, 1)

            def reciprocals(n, part):
                cols = slice(part * Q // RECIPS, (part + 1) * Q // RECIPS)
                dve.wait_ge(denom_copied, n + 1)
                nc.vector.reciprocal(recip[:, cols], denom[:, cols]).then_inc(recip_done, 1)

            def divide(n):
                dve.wait_ge(recip_done, (n + 1) * RECIPS)
                dve.wait_ge(context_copied, n + 1)
                dve.wait_ge(lo_done, n + 1)
                nc.vector.tensor_tensor(attn[:, :], context[:, :], recip[:, :], ALU.mult).then_inc(attn_done, 1)

            def middle(n, divided=True, more=True):
                for t in range(HEAD, NT):
                    for part, at in enumerate(RECIP_SLOTS):
                        if divided and at == t:
                            reciprocals(n - 1, part)
                    read_pairs(n + 1, range(BEFORE[t], BEFORE[t + 1]))
                    if t == TURN:
                        finish_max(n + 1)
                    if more:
                        read_pairs(n + 2, range(EARLY_BEFORE[t], EARLY_BEFORE[t + 1]))
                if divided:
                    divide(n - 1)
                for t in range(HEAD):
                    if more:
                        read_pairs(n + 2, range(BEFORE[t], BEFORE[t + 1]))
                    for h, at in enumerate(TAIL_SLOTS):
                        if at == t:
                            add_tail(n, h)

            dve.wait_ge(consts_ready, 2 + NS)
            read_pairs(0, range(PAIRS))
            finish_max(0)
            read_pairs(1, range(BEFORE[HEAD]))
            middle(0, divided=False)
            with dve.Fori(1, NG - 2) as n:
                middle(n)
            middle(NG - 2, more=False)
            for part in range(RECIPS):
                reciprocals(NG - 2, part)
            divide(NG - 2)
            for h in range(GH):
                add_tail(NG - 1, h)
            for part in range(RECIPS):
                reciprocals(NG - 1, part)
            divide(NG - 1)

        @block.tensor
        def _(pe):
            pe.sem_inc(context_done, NT)
            pe.sem_inc(denom_done, SB)

            def first_scores(n, s, q, load=None):
                u, half = divmod(q, 2)
                if q == 0:
                    pe.wait_ge(stacked[s], load * (LOADS * 16))
                if not (isinstance(n, int) and n * PAIRS + q < 2):
                    pe.wait_ge(first_read, n * PAIRS + q - 1)
                for c in (2 * half, 2 * half + 1):
                    last = nc.tensor.matmul(first[:, c, 0:CH], q_stack[s][0:S3, u * P:(u + 1) * P],
                                            k_stack[s][0:S3, c * CH:(c + 1) * CH], start=True, stop=True)
                last.then_inc(first_ready, 1)

            def second_scores(n, s, t, h):
                rows = P if t < NT - 1 else TL
                if t == 0 and h == 0:
                    pe.wait_ge(neg_stacked, (n + 1) * (P // HD) * 16)
                j = t * GH + h
                if j > HEAD * GH and BANK_OF[j] == 2 and 2 not in BANK_OF[HEAD * GH:j]:
                    if not (isinstance(n, int) and n == 0):
                        pe.wait_ge(denom_copied, n)
                else:
                    user = max(i for i in range(-2, j) if BANK_OF[i] == BANK_OF[j])
                    pe.wait_ge(exp_done, n * TILES + user + 1 + 2)
                nc.tensor.matmul(second[BANK_OF[j]][0:rows, :], k_stack[s][:, t * P:t * P + rows],
                                 q_stack[s][:, h * Q:(h + 1) * Q], start=True, stop=True).then_inc(second_ready, 1)

            def context_tile(n, s, t):
                rows = P if t < NT - 1 else TL
                pe.wait_ge(exp_done, exps(n, t))
                if t == 0 and not (isinstance(n, int) and n == 0):
                    pe.wait_ge(context_copied, n)
                for h in range(GH):
                    last = nc.tensor.matmul(context_ps[h * HD:(h + 1) * HD, :], values[s][0:rows, t * HD:(t + 1) * HD],
                                            probs[t][0:rows, h * Q:(h + 1) * Q], start=t == 0, stop=t == NT - 1)
                last.then_inc(context_done, 1)

            def denominators(n, i, direct=False):
                x, _ = BLOCKS[i]
                if x is None:
                    sources = [probs[NT - 2]]
                    pe.wait_ge(tail_added, (n + 1) * GH)
                elif direct:
                    sources = [probs[t] for t in RUNS[x]]
                    pe.wait_ge(exp_done, exps(n, RUNS[x][-1]))
                else:
                    sources = [run_sum[x]]
                    pe.wait_ge(added, (n + 1) * ADDS + ADDED_AT[RUNS[x][-1]])
                if i == 0:
                    user = max(j for j in range(TILES) if BANK_OF[j] == 2)
                    pe.wait_ge(exp_done, n * TILES + user + 1 + 2)
                for source in sources:
                    for h in range(GH):
                        last = nc.tensor.matmul(denom_ps[h * HD:(h + 1) * HD, :], ones[:, :],
                                                source[:, h * Q:(h + 1) * Q], start=i == 0, stop=i == SB - 1)
                last.then_inc(denom_done, 1)

            def slot(n, s, t, before=None, ahead=True, load=None, early=True):
                q = BEFORE[t]
                e = EARLY_BEFORE[t]
                for step in ORDER[t]:
                    if step == "P":
                        if ahead:
                            first_scores(n + 1, (s + 1) % NS, q, load)
                        q += 1
                    elif step == "N":
                        if early:
                            first_scores(n + 2, (s + 2) % NS, e, load)
                        e += 1
                    elif step == "C":
                        if t >= 1:
                            context_tile(n, s, t - 1)
                        elif before is not None:
                            context_tile(before, (s - 1) % NS, NT - 1)
                    elif step == "D":
                        for i, (_, at) in enumerate(BLOCKS):
                            if at == t:
                                denominators(n, i)
                            elif at == t + NT and before is not None:
                                denominators(before, i)
                    else:
                        second_scores(n, s, t, int(step))

            def group(i, s, ahead):
                n = i * BODY + s
                for t in range(HEAD, NT):
                    slot(n, s, t, ahead=ahead >= 1, load=i + (s + 2) // NS + 1, early=ahead >= 2)
                if ahead >= 1:
                    for t in range(HEAD):
                        slot(n + 1, (s + 1) % NS, t, before=n, ahead=ahead >= 2, load=i + (s + 2) // NS + 1)
                else:
                    for j, (run, _) in enumerate(BLOCKS):
                        if run is None:
                            context_tile(n, s, NT - 1)
                        denominators(n, j, direct=run == LAST_RUN)

            pe.wait_ge(consts_ready, 2 + NS)
            for q in range(PAIRS):
                first_scores(0, 0, q, 1)
            for q in range(EARLY):
                first_scores(1, 1, q, 1)
            for t in range(HEAD):
                slot(0, 0, t, load=1)
            with pe.Fori(0, PE_LOOPS) as i:
                for s in range(BODY):
                    group(i, s, 2)
            for n in range(PE_LOOPS * BODY, NG):
                group(n // BODY, n % BODY, NG - 1 - n)


def output(nc, a_scr, wo, ao, bo, x, out):
    QT, NN = Q // P, H // BANK
    UN = QT * NN
    with ExitStack() as ctx:
        sb = lambda n, s, d: ctx.enter_context(nc.sbuf_tensor(n, s, d))
        sem = lambda n: ctx.enter_context(nc.semaphore(n))
        parts = [sb(f"a_parts{i}", [P, NKV, 2 * Q], F32R) for i in range(2)]
        res = sb("res", [P, QT, H], F32)
        banks = [ctx.enter_context(nc.psum_tensor(f"o_bank{i}", [P, BANK], F32)) for i in range(UN)]
        fold = FoldedWeights(nc, ctx, "wo", H, [(ao, bo, wo, 0)], banks[QT:])
        w, UNITS = fold.parts, len(fold.units)
        assert UNITS == NN * KT and NN == 2
        a_loaded = [[sem(f"a_loaded{i}_{k}") for k in range(KT)] for i in range(2)]
        x_loaded, o_ready, o_added, o_stored = sem("res_loaded"), sem("o_ready"), sem("o_added"), sem("o_stored")
        block = ctx.enter_context(nc.Block())

        def tile_of(t, u):
            nn, qt = divmod(u, QT)
            return t[:, qt, nn * BANK:(nn + 1) * BANK]

        @block.sync
        def _(sp):
            def load(b, half, fold=None):
                sp.wait_ge(o_ready, (b + 1) * UN)
                for k in range(KT):
                    if fold:
                        fold.load(sp, k)
                    sp.dma_start(parts[half][:, k, :].bitcast(F32), a_scr[bass.ds(b * NKV + k, 1), :, :, :].rearrange(
                        "g p c q -> (g p) (c q)")).then_inc(a_loaded[half][k], 16)

            fold.load_lora(sp)
            load(0, 0, fold)
            for u in range(KT, UNITS):
                fold.load(sp, u)
            load(1, 1)
            with sp.Fori(1, B // 2) as bb:
                for half in range(2):
                    load(bb * 2 + half, half)

        @block.scalar
        def _(act):
            act.sem_inc(o_stored, UN * 16)
            for u in range(UNITS):
                fold.high(act, u)
            with act.Fori(0, B) as b:
                act.wait_ge(o_stored, (b + 1) * (UN * 16))
                act.dma_start(res[:, :, :], x[bass.ds(b, 1), :, :].rearrange(
                    "o (t p) n -> (o p) t n", p=P)).then_inc(x_loaded, 16)
                for u in range(UN):
                    act.wait_ge(o_added, b * UN + u + 1 + UN)
                    act.dma_start(tile_of(out[bass.ds(b, 1), :, :].rearrange("o (t p) n -> (o p) t n", p=P), u),
                                  tile_of(res, u)).then_inc(o_stored, 16)
            act.wait_ge(o_stored, (B + 1) * (UN * 16))

        @block.vector
        def _(dve):
            dve.sem_inc(o_added, UN)
            for u in range(UNITS):
                fold.add(dve, u)
                if u >= 1:
                    fold.low(dve, u - 1)
            fold.low(dve, UNITS - 1)
            with dve.Fori(0, B) as b:
                dve.wait_ge(x_loaded, (b + 1) * 16)
                for u in range(UN):
                    dve.wait_ge(o_ready, (b + 2) * UN + u + 1)
                    nc.vector.tensor_tensor(tile_of(res, u), banks[u][:, :], tile_of(res, u),
                                            ALU.add).then_inc(o_added, 1)

        @block.tensor
        def _(pe):
            def product(half, u, k):
                nn, qt = divmod(u, QT)
                for i, (xp, wp) in enumerate(TERMS):
                    q0 = xp * Q + qt * P
                    last = nc.tensor.matmul(banks[u][:, :], parts[half][:, k, q0:q0 + P],
                                            w[:, k, wp, nn * BANK:(nn + 1) * BANK], start=k == 0 and i == 0,
                                            stop=k == KT - 1 and i == len(TERMS) - 1)
                if k == KT - 1:
                    last.then_inc(o_ready, 1)

            def batch(bb, half):
                b = bb * 2 + half
                for u in range(UN):
                    pe.wait_ge(o_added, b * UN + u + 1)
                    for k in range(KT):
                        if u == 0:
                            pe.wait_ge(a_loaded[half][k], (bb + 1) * 16)
                        product(half, u, k)

            pe.sem_inc(o_ready, 2 * UN)
            for j in range(len(fold.banks)):
                fold.product(pe, j)
            for j, (k, c) in enumerate(fold.units):
                pe.wait_ge(fold.done, j + 1)
                if c == 0:
                    pe.wait_ge(a_loaded[0][k], 16)
                for u in range(c // BANK * QT, (c // BANK + 1) * QT):
                    if c and k == 0:
                        pe.wait_ge(fold.summed, UNITS - UN + u + 1)
                    product(0, u, k)
                if c == 0:
                    fold.product(pe, j + len(fold.banks))
                if j == KT - 1:
                    for rest in range(KT + len(fold.banks), UNITS):
                        fold.product(pe, rest)
            batch(0, 1)
            with pe.Fori(1, B // 2) as bb:
                for half in range(2):
                    batch(bb, half)


def build(nc, xT, x, ctxT, wq, aq, bq, wk, ak, bk, wv, av, bv, wo, ao, bo, out):
    k_scr = nc.dram_tensor("k_scr", (B * KV, 2, TP), F32).ap()
    v_scr = nc.dram_tensor("v_scr", (NG, P, NT * HD), F32).ap()
    q_scr = nc.dram_tensor("q_scr", (B * H, 2, Q), F32).ap()
    a_scr = nc.dram_tensor("a_scr", (NG, P, 2, Q), F32).ap()
    keys_and_values(nc, ctxT, wk, ak, bk, wv, av, bv, k_scr, v_scr)
    queries(nc, xT, wq, aq, bq, q_scr)
    attention(nc, k_scr, v_scr, q_scr, a_scr)
    output(nc, a_scr, wo, ao, bo, x, out)


def kernel(**inputs):
    import concourse.bacc as bacc
    from concourse.bass_utils import run_bass_kernel_spmd

    g = {k.replace("L0_xattn_", ""): np.asarray(v) for k, v in inputs.items()}
    ctx = g["ctx_4096"]
    arrays = {
        "xT": g["x"].transpose(0, 2, 1),
        "x": g["x"],
        "ctxT": np.pad(ctx, ((0, 0), (0, TP - T), (0, 0)), mode="edge").transpose(0, 2, 1),
    }
    for s in "qkvo":
        arrays[f"W{s}"], arrays[f"A{s}T"], arrays[f"B{s}"] = g[f"W{s}"], g[f"A{s}"].T, g[f"B{s}"]
    arrays = {f"in_{k}": np.ascontiguousarray(v) for k, v in arrays.items()}
    nc = bacc.Bacc("TRN2", target_bir_lowering=False, num_devices=1)
    args = [nc.dram_tensor(k, v.shape, mybir.dt.from_np(v.dtype), kind="ExternalInput").ap() for k, v in arrays.items()]
    out = nc.dram_tensor("out", (B, Q, H), F32, kind="ExternalOutput").ap()
    build(nc, *args, out)
    return run_bass_kernel_spmd(nc, [arrays], core_ids=[0]).results[0]["out"]
```
